# Optimizing a Trainium2 kernel written in Bass

```python
import numpy as np
import jax
import jax.numpy as jnp

def _softmax(x, axis=-1):
    return jax.nn.softmax(x, axis=axis)
def _gelu(x):
    return jax.nn.gelu(x, approximate=True)
def _silu(x):
    return jax.nn.silu(x)
def _sigmoid(x):
    return jax.nn.sigmoid(x)
def _layernorm(x, axis=-1, eps=1e-5):
    m = jnp.mean(x, axis=axis, keepdims=True)
    v = jnp.var(x, axis=axis, keepdims=True)
    return (x - m) / jnp.sqrt(v + eps)
def _scatter_add(tgt, idx, src, axis=0):
    return tgt.at[idx].add(src)
def _segment_sum(src, seg, n):
    return jax.ops.segment_sum(src, seg, n)

kernel_name = 'mk_conv_preact_d1_conv_nchw96_1ca507'

def setup_inputs(seed: int = 0):
    np.random.seed(seed)
    _w = jnp.asarray
    def _rec_inputs():
        import jax
        import jax.numpy as jnp
        _gk = jax.random.key(seed)
        x = -0.0001476 + 0.9999 * jax.random.normal(jax.random.fold_in(_gk, 1), (8, 96, 224, 224), jnp.float32)
        return x
    x = _rec_inputs()
    def _L0_conv_setup():
        import jax, jax.numpy as jnp
        import numpy as np
        WT_LEVELS = 3

        def haar2d(x):
            a = x[:, :, 0::2, 0::2]
            b = x[:, :, 0::2, 1::2]
            c = x[:, :, 1::2, 0::2]
            d = x[:, :, 1::2, 1::2]
            ll = (a + b + c + d) * 0.5
            lh = (a - b + c - d) * 0.5
            hl = (a + b - c - d) * 0.5
            hh = (a - b - c + d) * 0.5
            return jnp.stack([ll, lh, hl, hh], axis=2)

        def ihaar2d(co):
            ll, lh, hl, hh = (co[:, :, 0], co[:, :, 1], co[:, :, 2], co[:, :, 3])
            a = (ll + lh + hl + hh) * 0.5
            b = (ll - lh + hl - hh) * 0.5
            c = (ll + lh - hl - hh) * 0.5
            d = (ll - lh - hl + hh) * 0.5
            B, C, h, w = ll.shape
            top = jnp.stack([a, b], axis=-1).reshape(B, C, h, 2 * w)
            bot = jnp.stack([c, d], axis=-1).reshape(B, C, h, 2 * w)
            return jnp.stack([top, bot], axis=3).reshape(B, C, 2 * h, 2 * w)

        def dwconv(x, w):
            return jax.lax.conv_general_dilated(x, w, (1, 1), 'SAME', dimension_numbers=('NCHW', 'OIHW', 'NCHW'), feature_group_count=x.shape[1])
        key = jax.random.key(seed)
        ks = jax.random.split(key, 5)
        B, C, H, W, K, L = (8, 96, 224, 224, 5, WT_LEVELS)
        x = jax.random.normal(ks[0], (B, C, H, W), jnp.float32)
        base_w = jax.random.normal(ks[1], (C, 1, K, K), jnp.float32) * 0.1
        base_b = jax.random.normal(ks[2], (C,), jnp.float32) * 0.01
        base_scale = jnp.ones((1, C, 1, 1), jnp.float32)
        wconv_w = jax.random.normal(ks[3], (L, 4 * C, 1, K, K), jnp.float32) * 0.1
        wscale = jnp.full((L, 1, 4 * C, 1, 1), 0.1, jnp.float32)
        return {'x': x, 'base_w': base_w, 'base_b': base_b, 'base_scale': base_scale, 'wconv_w': wconv_w, 'wscale': wscale}
    _L0_conv_all = _L0_conv_setup()
    _L0_conv_in = {k: v for k, v in _L0_conv_all.items() if k in ('base_w', 'base_b', 'base_scale', 'wconv_w', 'wscale', )}
    del _L0_conv_all

    return {
        "x": x,
        "L0_conv_base_w": _L0_conv_in["base_w"],
        "L0_conv_base_b": _L0_conv_in["base_b"],
        "L0_conv_base_scale": _L0_conv_in["base_scale"],
        "L0_conv_wconv_w": _L0_conv_in["wconv_w"],
        "L0_conv_wscale": _L0_conv_in["wscale"],
    }

def reference(x, L0_conv_base_w, L0_conv_base_b, L0_conv_base_scale, L0_conv_wconv_w, L0_conv_wscale):
    import jax
    import jax.numpy as jnp
    def _L0_conv_ref(x, base_w, base_b, base_scale, wconv_w, wscale):
        import jax, jax.numpy as jnp
        import numpy as np
        WT_LEVELS = 3

        def haar2d(x):
            a = x[:, :, 0::2, 0::2]
            b = x[:, :, 0::2, 1::2]
            c = x[:, :, 1::2, 0::2]
            d = x[:, :, 1::2, 1::2]
            ll = (a + b + c + d) * 0.5
            lh = (a - b + c - d) * 0.5
            hl = (a + b - c - d) * 0.5
            hh = (a - b - c + d) * 0.5
            return jnp.stack([ll, lh, hl, hh], axis=2)

        def ihaar2d(co):
            ll, lh, hl, hh = (co[:, :, 0], co[:, :, 1], co[:, :, 2], co[:, :, 3])
            a = (ll + lh + hl + hh) * 0.5
            b = (ll - lh + hl - hh) * 0.5
            c = (ll + lh - hl - hh) * 0.5
            d = (ll - lh - hl + hh) * 0.5
            B, C, h, w = ll.shape
            top = jnp.stack([a, b], axis=-1).reshape(B, C, h, 2 * w)
            bot = jnp.stack([c, d], axis=-1).reshape(B, C, h, 2 * w)
            return jnp.stack([top, bot], axis=3).reshape(B, C, 2 * h, 2 * w)

        def dwconv(x, w):
            return jax.lax.conv_general_dilated(x, w, (1, 1), 'SAME', dimension_numbers=('NCHW', 'OIHW', 'NCHW'), feature_group_count=x.shape[1])
        B, C, H, W = x.shape
        cur = x
        level_coeffs = []
        for i in range(WT_LEVELS):
            co = haar2d(cur)
            cur = co[:, :, 0]
            h, w = co.shape[-2:]
            flat = co.reshape(B, C * 4, h, w)
            flat = dwconv(flat, wconv_w[i]) * wscale[i]
            level_coeffs.append(flat.reshape(B, C, 4, h, w))
        next_ll = jnp.zeros_like(level_coeffs[-1][:, :, 0])
        for i in reversed(range(WT_LEVELS)):
            co = level_coeffs[i].at[:, :, 0].add(next_ll)
            next_ll = ihaar2d(co)
        base = dwconv(x, base_w) * base_scale + base_b.reshape(1, C, 1, 1)
        return base + next_ll

    def _gn(v, G=32, eps=1e-5):
        B_, C_, H_, W_ = v.shape
        g = v.reshape(B_, G, C_ // G, H_, W_)
        m = jnp.mean(g, axis=(2, 3, 4), keepdims=True)
        s = jnp.var(g, axis=(2, 3, 4), keepdims=True)
        return ((g - m) / jnp.sqrt(s + eps)).reshape(v.shape)

    def _ln_c(v, eps=1e-6):
        m = jnp.mean(v, axis=1, keepdims=True)
        s = jnp.var(v, axis=1, keepdims=True)
        return (v - m) / jnp.sqrt(s + eps)

    def _ln_t(v, eps=1e-5):
        m = jnp.mean(v, axis=-1, keepdims=True)
        s = jnp.var(v, axis=-1, keepdims=True)
        return (v - m) / jnp.sqrt(s + eps)

    def _to_tokens(v):
        B_, C_, H_, W_ = v.shape
        return v.reshape(B_, C_, H_ * W_).transpose(0, 2, 1)
    def _from_tokens(t, like):
        B_, C_, H_, W_ = like.shape
        return t.transpose(0, 2, 1).reshape(B_, C_, H_, W_)

    x = x + _L0_conv_ref(_gn(x), L0_conv_base_w, L0_conv_base_b, L0_conv_base_scale, L0_conv_wconv_w, L0_conv_wscale)
    return x


_drawn_inputs = setup_inputs


def setup_inputs(seed=0):
    import zlib

    import numpy as np

    out = dict(_drawn_inputs(seed))
    spreads = {'L0_conv_base_scale': (1.0, 0.2), 'L0_conv_wscale': (0.10000000149011612, 0.6)}
    factors = {'L0_conv_base_b': 6.488}
    for name, (base, spread) in spreads.items():
        noise = np.random.default_rng([zlib.crc32(name.encode()), seed]).standard_normal(out[name].shape)
        drawn = base * np.exp(spread * noise) if base else spread * noise
        out[name] = jnp.asarray(drawn.astype(out[name].dtype))
    for name, factor in factors.items():
        out[name] = (out[name] * factor).astype(out[name].dtype)
    return out
```

```python
from contextlib import ExitStack

import concourse.bass as bass
from concourse import mybir



def build(nc, x, base_w, base_b, base_scale, wconv_w, wscale, ident_c, avg_c, mask_c, out):
    f32 = mybir.dt.float32
    f16 = mybir.dt.float16
    ALU = mybir.AluOpType
    ACT = mybir.ActivationFunctionType

    B, C, H, W = x.shape
    GC = 3
    G = C // GC
    RC, CC = 8, 16
    KS = 5
    REACH = 4
    WIN_R, WIN_C = RC + 2 * REACH, CC + 2 * REACH
    PATCH = 2 * KS
    PAD_R, PAD_C = RC - 2, CC - 2
    TAB_R, TAB_C = PATCH + 2 * PAD_R, PATCH + 2 * PAD_C
    LV = 3
    S_X, S_W = 4.0, 256.0
    HALVES = 2
    IMG = B // HALVES
    PITCH = 32
    CR = H // RC
    NB = W // CC
    HB = NB // 2
    HC = W // 2
    ROW = RC * W
    UNITS = 6
    SLOTS = 6
    AHEAD = 2
    TURNS = C // SLOTS
    EPS = 1e-5
    Q4 = 4 * HC
    MEAN_UNIT, VAR_UNIT = 3, 4
    MEAN_AT, VAR_AT = 508, 510

    ctx = ExitStack()
    with ctx:
        def sb(name, shape, dt=f32):
            return ctx.enter_context(nc.sbuf_tensor(name, shape, dt))

        def sem(name):
            return ctx.enter_context(nc.semaphore(name))

        X = sb("X", [128, SLOTS, HALVES, ROW])
        XN = sb("XN", [128, 2, HALVES, ROW])
        RS = sb("RS", [128, ROW // 2])
        D1 = sb("D1", [128, HALVES, Q4])
        D1p = sb("D1p", [128, 2 * Q4])
        B1 = sb("B1", [128, 2 * Q4])
        RS2 = sb("RS2", [128, Q4])
        D2 = sb("D2", [128, Q4 // 2])
        D2p = sb("D2p", [64, Q4])
        B2 = sb("B2", [128, 4, RC, CC])
        XH = sb("XH", [128, HALVES, NB, 130], f16)
        XL = sb("XL", [128, HALVES, NB, 130], f16)
        XH1 = sb("XH1", [128, HB, 130], f16)
        XL1 = sb("XL1", [128, HB, 130], f16)
        XH2 = sb("XH2", [128, 4, 66], f16)
        XL2 = sb("XL2", [128, 4, 66], f16)
        TW = sb("TW", [128, 2, LV, WIN_R, WIN_C, 2, GC], f16)
        N2q = sb("N2q", [64, Q4])
        N2m = sb("N2m", [128, Q4 // 2])
        N1r = sb("N1r", [128, 2 * Q4])
        N1m = sb("N1m", [128, HALVES, Q4])
        ident = sb("ident", [128, 128])
        avg = sb("avg", [128, 128])
        mask = sb("mask", [128, 1])
        bias = sb("bias", [128, C])
        ST = sb("ST", [128, HALVES, GC * 4, 6])
        MV = sb("MV", [128, HALVES, 2])
        GM = sb("GM", [128, HALVES])
        SQ = sb("SQ", [128, 4, HALVES])
        RG = sb("RG", [128, HALVES])
        spare = sb("spare", [128, 1])
        ZT = sb("ZT", [PATCH * PATCH, LV * 4, G, 2 * GC], f16)

        O = [[ctx.enter_context(nc.psum_tensor(f"O{p}{b}", [128, 512], f32)) for b in range(2)] for p in range(2)]
        S = [[ctx.enter_context(nc.psum_tensor(f"S{p}{b}", [128, 512], f32)) for b in range(2)] for p in range(2)]

        xn_flat = XN[:, :, :, :].rearrange("p a h n -> p (a h n)")
        off = [0]

        def carve(n):
            off[0] += n
            return xn_flat[0:C, off[0] - n:off[0]]

        WCf, AAf, HHf = carve(LV * 4 * 25), carve(LV * 4 * 25), carve(LV * 4 * 25)
        BWf, WSf, BSf, ZZf = carve(25), carve(LV * 4), carve(1), carve(LV * 4 * PATCH * PATCH)
        zero_n = LV * G * 4 * TAB_R * TAB_C * 2 * GC // 128 // 2
        zeros = xn_flat[:, off[0] + 1:off[0] + 1 + zero_n // 2].bitcast(f16)

        table = nc.dram_tensor("table", [LV, G, 4, TAB_R, TAB_C, 2 * GC], f16, kind="Internal")

        consts_in = sem("consts_in")
        weights_in = sem("weights_in")
        cleared = sem("cleared")
        zeros_ready = sem("zeros_ready")
        pads_clear = sem("pads_clear")
        table_zero = sem("table_zero")
        table_first = sem("table_first")
        table_next = sem("table_next")
        table_rest = sem("table_rest")
        chain = sem("chain")
        z_ready = sem("z_ready")
        z_turned = sem("z_turned")
        z_high = sem("z_high")
        z_low = sem("z_low")
        x_in = [sem(f"x_in{s}") for s in range(SLOTS)]
        stored = [sem(f"stored{s}") for s in range(SLOTS)]
        tw_in = [sem(f"tw_in{s}") for s in range(2)]
        mv_ready = sem("mv_ready")
        vq_ready = sem("vq_ready")
        xn_done = sem("xn_done")
        d1_done = sem("d1_done")
        rs_done = sem("rs_done")
        d1p_in = sem("d1p_in")
        b1_done = sem("b1_done")
        d2_done = sem("d2_done")
        d2p_in = sem("d2p_in")
        b2_done = sem("b2_done")
        turned = sem("turned")
        high = sem("high")
        low = sem("low")
        mm_done = sem("mm_done")
        fin = sem("fin")
        n2q_done = sem("n2q_done")
        rs2_done = sem("rs2_done")
        stat_step = sem("stat_step")
        root_done = sem("root_done")
        var_first = sem("var_first")
        stat_mm = sem("stat_mm")
        n1r_evac = sem("n1r_evac")
        n2m_in = sem("n2m_in")
        n1r_done = sem("n1r_done")
        n1m_in = sem("n1m_in")
        xadd_done = sem("xadd_done")

        block = ctx.enter_context(nc.Block())

        def wait(eng, s, per_channel, i, k, const=0):
            v = i * (per_channel * SLOTS) + (per_channel * k + const)
            if not isinstance(v, int) or v > 0:
                eng.wait_ge(s, v)

        def count(per_channel, i, k, const=0):
            return i * (per_channel * SLOTS) + (per_channel * k + const)

        XDMA = 16 * B
        TWDMA = 16 * LV * RC * 2

        def first_of(i, k):
            return isinstance(i, int) and i == 0 and k == 0

        def past_end(i, k):
            return isinstance(i, int) and i * SLOTS + k >= C

        @block.sync
        def _(sp):
            def held(value):
                return value if isinstance(value, int) else sp.compute_val(value)

            def held_address(elements, size):
                at = held(elements)
                held(at * size)
                return at

            def wait_held(s, value):
                if not isinstance(value, int) or value > 0:
                    sp.wait_ge(s, value)

            def plane(t, b, at):
                return bass.AP(t.tensor, at + b * C * H * W, [[ROW, CR], [1, ROW]])

            def load_x(i, k):
                s = k % SLOTS
                at = held_address((i * SLOTS + k) * (H * W), 4)
                before = held(count(0, 0, 0, (i + k // SLOTS) * XDMA))
                wait_held(stored[s], before)
                for b in range(B):
                    h, bb = b // IMG, b % IMG
                    sp.dma_start(X[PITCH * bb:PITCH * bb + CR, s, h, :], plane(x, b, at)).then_inc(x_in[s], 16)

            def store_x(i, k):
                s = k % SLOTS
                at = held_address((i * SLOTS + k) * (H * W), 4)
                full = held(count(1, i, k, 1))
                wait_held(xadd_done, full)
                for b in range(B):
                    h, bb = b // IMG, b % IMG
                    sp.dma_start(plane(out, b, at), X[PITCH * bb:PITCH * bb + CR, s, h, :]).then_inc(stored[s], 16)

            def load_tw(gk, i):
                buf = gk % 2
                size = 4 * TAB_R * TAB_C * 2 * GC
                corner = PAD_R * TAB_C * 2 * GC
                at = held_address((i * 2 + gk) * size + corner, 2)
                freed = held(count(UNITS, i, GC * (gk - 1)))
                wait_held(mm_done, freed)
                for lv in range(LV):
                    for r in range(RC):
                        P, pr = r // 2, r % 2
                        for pc in range(2):
                            fixed = ((lv * G * 4 + 2 * pr + pc) * TAB_R - 2 * P) * TAB_C * 2 * GC
                            src = bass.AP(table, at + fixed, [[2 * 2 * GC, CC // 2], [TAB_C * 2 * GC, WIN_R],
                                                              [1, WIN_C * 2 * GC]])
                            dst = TW[CC * r + pc:CC * r + CC:2, buf, lv, :, :, :, :]
                            sp.dma_start(dst.rearrange("p r c a s -> p r (c a s)"), src).then_inc(tw_in[buf], 16)

            def d1_move(i, k):
                v, w = held(count(1, i, k, 1)), held(count(1, i, k))
                wait_held(d1_done, v)
                wait_held(b1_done, w)
                wait_held(d2_done, w)
                for h in range(HALVES):
                    sp.dma_start(D1p[64 * h:64 * h + 64, :], D1[:, h, :]).then_inc(d1p_in, 16)

            def d2_move(i, k):
                v, w = held(count(1, i, k, 1)), held(count(1, i, k))
                wait_held(d2_done, v)
                wait_held(b2_done, w)
                sp.dma_start(D2p[:, :], D2[:, :]).then_inc(d2p_in, 16)

            def n2_move(i, k):
                v, w = held(count(1, i, k, 1)), held(count(1, i, k))
                wait_held(n2q_done, v)
                wait_held(n1r_done, w)
                sp.dma_start(N2m[:, :], N2q[:, :]).then_inc(n2m_in, 16)

            def n1_move(i, k):
                v, w = held(count(1, i, k, 1)), held(count(1, i, k))
                wait_held(n1r_done, v)
                wait_held(xadd_done, w)
                for h in range(HALVES):
                    sp.dma_start(N1m[:, h, :], N1r[64 * h:64 * h + 64, :]).then_inc(n1m_in, 16)

            sp.dma_start(WCf.rearrange("c (l n) -> c l n", l=LV),
                         wconv_w.rearrange("l (c s) a b -> c l (s a b)", s=4)).then_inc(weights_in, 16)
            sp.dma_start(BWf, base_w.rearrange("c a b -> c (a b)")).then_inc(weights_in, 16)
            sp.dma_start(WSf.rearrange("c (l n) -> c l n", l=LV),
                         wscale.rearrange("l (c s) -> c l s", s=4)).then_inc(weights_in, 16)
            sp.dma_start(BSf, base_scale.rearrange("(c o) -> c o", o=1)).then_inc(weights_in, 16)
            sp.dma_start(ident[:, :], ident_c).then_inc(consts_in, 16)
            sp.dma_start(avg[:, :], avg_c).then_inc(consts_in, 16)
            sp.dma_start(mask[:, :], mask_c).then_inc(consts_in, 16)
            sp.dma_start(bias[:, :], base_b.partition_broadcast(128)).then_inc(consts_in, 16)
            sp.wait_ge(cleared, 3)
            for k in range(GC):
                load_x(0, k)
            flat = table.ap().rearrange("l g q r c n -> (l g q r c n)").rearrange("(a p n) -> a p n", a=2, p=128)
            sp.wait_ge(zeros_ready, 1)
            for a in range(2):
                sp.dma_start(flat[a], zeros).then_inc(table_zero, 16)
            load_x(0, GC)
            sp.wait_ge(table_zero, 32)
            sp.wait_ge(z_low, LV)
            def write_table(g0, g1, s):
                for lv in range(LV):
                    for q in range(4):
                        stored_q = 2 * (q // 2) + 1 - q % 2
                        for a in range(PATCH):
                            dst = table.ap()[lv, g0:g1, stored_q, PAD_R + a, PAD_C:PAD_C + PATCH, :]
                            sp.dma_start(dst.rearrange("g c n -> c g n"),
                                         ZT[PATCH * a:PATCH * a + PATCH, 4 * lv + q, g0:g1, :]).then_inc(s, 16)

            TABLE = 16 * LV * 4 * PATCH
            FIRST = 2
            PART = (G - FIRST) // SLOTS
            write_table(0, FIRST, table_first)
            sp.wait_ge(table_first, TABLE)
            load_tw(0, 0)
            d1_move(0, 0)
            load_tw(1, 0)
            d2_move(0, 0)

            def turn(i):
                for k in range(SLOTS):
                    if not first_of(i, k):
                        n2_move(i, k - 1)
                        n1_move(i, k - 1)
                    if not past_end(i, k + 1):
                        d1_move(i, k + 1)
                    if not past_end(i, k + 4):
                        load_x(i, k + 4)
                    if not first_of(i, k):
                        store_x(i, k - 1)
                    if not past_end(i, k + 1):
                        d2_move(i, k + 1)
                    if isinstance(i, int) and i == 0:
                        write_table(FIRST + PART * k, FIRST + PART * (k + 1), table_rest if k else table_next)
                    if k % GC == 0 and not past_end(i, k + GC) and not first_of(i, k):
                        if isinstance(i, int) and i == 0:
                            sp.wait_ge(table_next, TABLE)
                        else:
                            sp.wait_ge(table_rest, TABLE * (SLOTS - 1))
                        load_tw(k // GC + 1, i)

            turn(0)
            with sp.Fori(1, TURNS - 1) as i:
                turn(i)
            turn(TURNS - 1)
            n2_move(TURNS, -1)
            n1_move(TURNS, -1)
            store_x(TURNS, -1)
            for s in range(SLOTS):
                sp.wait_ge(stored[s], TURNS * XDMA)

        @block.gpsimd
        def _(pool):
            nc.gpsimd.memset(X[:, 4:6, :, :], 0.0).then_inc(cleared, 1)

            def d1_sum(i, k):
                wait(pool, xn_done, 1, i, k, 1)
                wait(pool, d1p_in, 32, i, k)
                for h in range(HALVES):
                    if h == 0:
                        wait(pool, d1_done, 1, i, k)
                    else:
                        wait(pool, rs_done, 3, i, k, 2)
                    v = XN[:, k % 2, h, :].rearrange("p (jr two c) -> p jr two c", two=2, c=CC)
                    nc.gpsimd.tensor_tensor(RS[:, :].rearrange("p (jr c) -> p jr c", c=CC), v[:, :, 0, :],
                                            v[:, :, 1, :], ALU.add).then_inc(rs_done, 1)
                    wait(pool, rs_done, 3, i, k, 2 * h + 1)
                    t = RS[:, :].rearrange("p (j r q two) -> p r j q two", j=NB, r=4, two=2)
                    o = D1[:, h, :].rearrange("p (r j q) -> p r j q", r=4, q=CC // 2)[:, :, :, ::-1]
                    nc.gpsimd.tensor_tensor(o, t[:, :, :, :, 0], t[:, :, :, :, 1],
                                            ALU.add).then_inc(d1_done if h else rs_done, 1)

            def d2_sum(i, k):
                wait(pool, d1p_in, 32, i, k, 32)
                wait(pool, d2p_in, 16, i, k)
                v = D1p[:, :].rearrange("p (r two c) -> p r two c", two=2, c=HC)
                nc.gpsimd.tensor_tensor(RS2[:, :].rearrange("p (r c) -> p r c", r=4), v[:, :, 0, :], v[:, :, 1, :],
                                        ALU.add).then_inc(rs2_done, 1)
                wait(pool, rs2_done, 1, i, k, 1)
                t = RS2[:, :].rearrange("p (n two) -> p n two", two=2)
                nc.gpsimd.tensor_tensor(D2[:, :], t[:, :, 0], t[:, :, 1], ALU.add).then_inc(d2_done, 1)

            def up(v, cols):
                return v.rearrange("p (r c o) -> p r c o", r=4, o=1).to_broadcast([128, 4, cols, 2])

            def n1_add(i, k):
                wait(pool, n2m_in, 16, i, k, 16)
                wait(pool, n1r_evac, 1, i, k, 1)
                v = N1r[:, :].rearrange("p (r two c d) -> p r two c d", two=2, c=HC // 2, d=2)
                for a in range(2):
                    op = nc.gpsimd.tensor_tensor(v[:, :, a, :, :], v[:, :, a, :, :], up(N2m[:, :], HC // 2), ALU.add)
                op.then_inc(n1r_done, 1)

            def x_add(i, k):
                wait(pool, n1m_in, 32, i, k, 32)
                wait(pool, fin, 4, i, k, 4)
                for h in range(HALVES):
                    v = X[:, k % SLOTS, h, :].rearrange("p (r two c d) -> p r two c d", two=2, c=HC, d=2)
                    for a in range(2):
                        op = nc.gpsimd.tensor_tensor(v[:, :, a, :, :], v[:, :, a, :, :], up(N1m[:, h, :], HC), ALU.add)
                op.then_inc(xadd_done, 1)

            d1_sum(0, 0)
            d2_sum(0, 0)

            def turn(i):
                for k in range(SLOTS):
                    if not first_of(i, k):
                        n1_add(i, k - 1)
                    if not past_end(i, k + 1):
                        d1_sum(i, k + 1)
                    if not first_of(i, k):
                        x_add(i, k - 1)
                    if not past_end(i, k + 1):
                        d2_sum(i, k + 1)

            turn(0)
            with pool.Fori(1, TURNS - 1) as i:
                turn(i)
            turn(TURNS - 1)
            n1_add(TURNS, -1)
            x_add(TURNS, -1)

        def split_dst(u, hi):
            if u < 4:
                h, c = u // 2, u % 2
                return (XH if hi else XL)[:, h, HB * c:HB * c + HB, 1:129]
            if u == 4:
                return (XH2 if hi else XL2)[:, :, 1:65]
            return (XH1 if hi else XL1)[:, :, 1:129]

        def banks(u):
            return [(0, 2), (2, 4)] if u == 4 else [(0, 4), (4, 7)]

        def rows_of(u):
            return 64 if u == 4 else 128

        def split_wait(eng, u, i, k):
            last = (2, 2, 4, 4, 5, 6)[u] - UNITS
            wait(eng, mm_done, UNITS, i, k, last)

        @block.scalar
        def _(act):
            nc.scalar.memzero(X[:, 2:4, :, :]).then_inc(cleared, 1)
            for lv in range(LV):
                act.wait_ge(z_turned, lv + 1)
                src = S[lv // 2][lv % 2][0:PATCH * PATCH, 0:4 * C].rearrange("p (q s) -> p q s", s=GC)
                dst = ZT[:, 4 * lv:4 * lv + 4, :, 0:GC].rearrange("p q g s -> p (q g) s")
                nc.scalar.activation(dst, src, ACT.Copy).then_inc(z_high, 1)

            def high_part(i, k, u):
                split_wait(act, u, i, k)
                for b, (j0, j1) in enumerate(banks(u)):
                    wait(act, turned, 2 * UNITS, i, k, 2 * u + b + 1)
                    src = S[u % 2][b][:, 0:(j1 - j0) * 128].rearrange("p (j m) -> p j m", m=128)[:, :, 0:rows_of(u)]
                    nc.scalar.activation(split_dst(u, True)[:, j0:j1, :], src, ACT.Copy).then_inc(high, 1)

            def b1_copy(i, k):
                wait(act, d1p_in, 32, i, k, 32)
                wait(act, turned, 2 * UNITS, i, k - 1, 2 * UNITS)
                src = D1p[:, :].rearrange("p (r j c) -> p r j c", r=RC, c=CC)
                dst = B1[:, :].rearrange("p (j r c) -> p r j c", r=RC, c=CC)[:, :, :, ::-1]
                nc.scalar.activation(dst, src, ACT.Copy).then_inc(b1_done, 1)

            def b2_copy(i, k):
                wait(act, d2p_in, 16, i, k, 16)
                wait(act, turned, 2 * UNITS, i, k - 1, 2 * UNITS - 2)
                v = D2p[:, :].rearrange("p (r c) -> p r c", r=RC)
                src = v[:, :, 0:48].rearrange("p r (j c) -> p r j c", c=CC)
                dst = B2[0:64, 0:3, :, :].rearrange("p j r c -> p r j c")[:, :, :, ::-1]
                nc.scalar.activation(dst, src, ACT.Copy)
                nc.scalar.activation(B2[0:64, 3, :, 8:16][:, :, ::-1], v[:, :, 48:56], ACT.Copy).then_inc(b2_done, 1)

            def n2_evac(i, k):
                wait(act, mm_done, UNITS, i, k, 5)
                wait(act, n2m_in, 16, i, k)
                for b in range(2):
                    op = nc.scalar.activation(N2q[:, b * 224:b * 224 + 224], O[0][b][0:64, 0:224], ACT.Copy,
                                              scale=0.25 / (4 * S_X * S_W))
                op.then_inc(n2q_done, 1)

            def n1_evac(i, k):
                wait(act, mm_done, UNITS, i, k, 6)
                wait(act, n1m_in, 32, i, k)
                for b in range(2):
                    op = nc.scalar.activation(N1r[:, b * Q4:b * Q4 + Q4], O[1][b][:, 0:Q4], ACT.Identity,
                                              scale=0.5 / (2 * S_X * S_W), bias=bias[:, bass.ds(i * SLOTS + k, 1)])
                op.then_inc(n1r_evac, 1)

            def root():
                nc.scalar.activation(SQ[:, 1, :], SQ[:, 0, :], ACT.Sqrt).then_inc(root_done, 1)

            act.wait_ge(var_first, 1)
            root()
            act.wait_ge(pads_clear, 7)
            act.wait_ge(consts_in, 64)
            b1_copy(0, 0)
            b2_copy(0, 0)
            for u in range(AHEAD):
                high_part(0, 0, u)

            def turn(i):
                for k in range(SLOTS):
                    for u in range(UNITS):
                        v = u + AHEAD
                        if not past_end(i, k + v // UNITS):
                            high_part(i, k + v // UNITS, v % UNITS)
                        if v == VAR_UNIT and k % GC == GC - 1 and not past_end(i, k + 1):
                            wait(act, low, 2 * UNITS, i, k, 2 * v + 2)
                            root()
                        if u == 3 and not past_end(i, k + 1):
                            b1_copy(i, k + 1)
                        if u == 4:
                            n2_evac(i, k)
                    n1_evac(i, k)
                    if not past_end(i, k + 1):
                        b2_copy(i, k + 1)

            turn(0)
            with act.Fori(1, TURNS - 1) as i:
                turn(i)
            turn(TURNS - 1)

        @block.vector
        def _(dve):
            links = [0]

            def link(op):
                links[0] += 1
                op.then_inc(chain, 1)
                dve.wait_ge(chain, links[0])

            nc.vector.memset(X[:, 0:2, :, :], 0.0).then_inc(cleared, 1)
            nc.vector.memset(zeros, 0.0).then_inc(zeros_ready, 1)
            for t in (XH, XL):
                nc.vector.memset(t[:, :, :, :], 0.0).then_inc(pads_clear, 1)
            for t in (XH1, XL1, XH2, XL2):
                nc.vector.memset(t[:, :, :], 0.0).then_inc(pads_clear, 1)
            nc.vector.memset(B2[:, :, :, :], 0.0).then_inc(pads_clear, 1)

            dve.wait_ge(weights_in, 64)
            WC = WCf.rearrange("c (ls n) -> c ls n", n=25)
            link(nc.vector.tensor_tensor(WC, WC, WSf.rearrange("c (ls o) -> c ls o", o=1)
                                         .to_broadcast([C, LV * 4, 25]), ALU.mult))
            W4 = WCf.rearrange("c (lp two n) -> c lp two n", two=2, n=25)
            A4 = AAf.rearrange("c (lp two n) -> c lp two n", two=2, n=25)
            link(nc.vector.tensor_tensor(A4[:, :, 0, :], W4[:, :, 0, :], W4[:, :, 1, :], ALU.add))
            link(nc.vector.tensor_tensor(A4[:, :, 1, :], W4[:, :, 0, :], W4[:, :, 1, :], ALU.subtract))
            A2 = AAf.rearrange("c (l two n) -> c l two n", l=LV, two=2)
            H2 = HHf.rearrange("c (l two n) -> c l two n", l=LV, two=2)
            link(nc.vector.tensor_tensor(H2[:, :, 0, :], A2[:, :, 0, :], A2[:, :, 1, :], ALU.add))
            link(nc.vector.tensor_tensor(H2[:, :, 1, :], A2[:, :, 0, :], A2[:, :, 1, :], ALU.subtract))
            HV = HHf.rearrange("c (l x a b) -> c l x a b", l=LV, x=4, a=KS)
            Z = ZZf.rearrange("c (l q a b) -> c l q a b", l=LV, q=4, a=PATCH)
            for q in range(4):
                for o in range(4):
                    link(nc.vector.tensor_scalar(Z[:, :, q, o // 2::2, o % 2::2], HV[:, :, q ^ o, :, :],
                                                 0.25 * S_W, None, ALU.mult))
            BW = BWf.rearrange("c (a b) -> c a b", a=KS)
            link(nc.vector.tensor_scalar(BWf, BWf, BSf, S_W, ALU.mult, ALU.mult))
            for q in range(4):
                t = Z[:, 0, q, q // 2 + 2:q // 2 + 2 + KS, q % 2 + 2:q % 2 + 2 + KS]
                op = nc.vector.tensor_tensor(t, t, BW, ALU.add)
                if q == 3:
                    op.then_inc(z_ready, 1)
                else:
                    link(op)
            for lv in range(LV):
                dve.wait_ge(z_high, lv + 1)
                src = S[lv // 2][lv % 2][0:PATCH * PATCH, 0:4 * C].rearrange("p (q s) -> p q s", s=GC)
                z = ZT[:, 4 * lv:4 * lv + 4, :, :].rearrange("p q g s -> p (q g) s")
                nc.vector.tensor_tensor(z[:, :, GC:2 * GC], src, z[:, :, 0:GC], ALU.subtract).then_inc(z_low, 1)

            def chan_stats(i, k, h):
                dve.wait_ge(x_in[k % SLOTS], (i + k // SLOTS + 1) * XDMA)
                for c in range(4):
                    op = nc.vector.bn_stats(ST[:, h, 4 * (k % GC) + c, :], X[:, k % SLOTS, h, c * Q4:(c + 1) * Q4])
                return op

            STEPS = 8

            def step(op, i, gk, n):
                op.then_inc(stat_step, 1)
                dve.wait_ge(stat_step, i * (2 * STEPS) + (gk * STEPS + n))

            def stats_mean(last, i, gk):
                step(last, i, gk, 1)
                nc.vector.memset(spare[:, :], 0.0)
                for h in range(HALVES):
                    op = nc.vector.bn_aggr(MV[:, h, :], ST[:, h, :, :].rearrange("p a b -> p (a b)"))
                op.then_inc(mv_ready, 1)

            def take_mean(bank):
                return nc.vector.tensor_copy(GM[:, :], bank[:, MEAN_AT:MEAN_AT + HALVES])

            def stats_var(i, gk):
                step(nc.vector.tensor_tensor(SQ[:, 0, :], MV[:, :, 0], GM[:, :], ALU.subtract), i, gk, 2)
                step(nc.vector.tensor_tensor(SQ[:, 1, :], SQ[:, 0, :], SQ[:, 0, :], ALU.mult), i, gk, 3)
                nc.vector.tensor_tensor(SQ[:, 2, :], SQ[:, 1, :], MV[:, :, 1], ALU.add).then_inc(vq_ready, 1)

            def take_var(bank):
                return nc.vector.tensor_scalar(SQ[:, 0, :], bank[:, VAR_AT:VAR_AT + HALVES], EPS, None, ALU.add)

            def stats_scale(i, gk):
                dve.wait_ge(root_done, i * 2 + (gk + 1))
                step(nc.vector.reciprocal(SQ[:, 1, :], SQ[:, 1, :]), i, gk, 4)
                step(nc.vector.tensor_tensor(SQ[:, 3, :], SQ[:, 1, :], SQ[:, 1, :], ALU.mult), i, gk, 5)
                step(nc.vector.tensor_tensor(SQ[:, 3, :], SQ[:, 3, :], SQ[:, 0, :], ALU.mult), i, gk, 6)
                step(nc.vector.tensor_scalar(SQ[:, 3, :], SQ[:, 3, :], -0.5, 1.5, ALU.mult, ALU.add), i, gk, 7)
                step(nc.vector.scalar_tensor_tensor(RG[:, :], SQ[:, 1, :], mask[:, 0:1], SQ[:, 3, :], ALU.mult,
                                                    ALU.mult), i, gk, 8)

            def normalise(i, k):
                wait(dve, turned, 2 * UNITS, i, k - 2, 8)
                wait(dve, d1_done, 1, i, k - 1)
                for h in range(HALVES):
                    src = X[:, k % SLOTS, h, :].rearrange("p (r j c) -> p r j c", r=RC, c=CC)
                    dst = XN[:, k % 2, h, :].rearrange("p (j r c) -> p r j c", r=RC, c=CC)[:, :, :, ::-1]
                    op = nc.vector.tensor_scalar(dst, src, GM[:, h:h + 1], RG[:, h:h + 1], ALU.subtract, ALU.mult)
                op.then_inc(xn_done, 1)

            def low_part(i, k, u):
                for b, (j0, j1) in enumerate(banks(u)):
                    wait(dve, high, 2 * UNITS, i, k, 2 * u + b + 1)
                    src = S[u % 2][b][:, 0:(j1 - j0) * 128].rearrange("p (j m) -> p j m", m=128)[:, :, 0:rows_of(u)]
                    op = nc.vector.tensor_tensor(split_dst(u, False)[:, j0:j1, :], src,
                                                 split_dst(u, True)[:, j0:j1, :], ALU.subtract)
                    if b == 0:
                        op.then_inc(low, 1)
                return op

            def final(i, k, u):
                wait(dve, mm_done, UNITS, i, k, u + 1)
                h, c = u // 2, u % 2
                for b in range(2):
                    t = X[:, k % SLOTS, h, :].rearrange("p (b r w) -> p b r w", b=2, r=4)[:, b, :, HC * c:HC * c + HC]
                    op = nc.vector.scalar_tensor_tensor(t, O[u % 2][b][:, 0:Q4].rearrange("p (r w) -> p r w", r=4),
                                                        1.0 / (S_X * S_W), t, ALU.mult, ALU.add)
                op.then_inc(fin, 1)

            dve.wait_ge(consts_in, 64)
            for k in range(GC):
                for h in range(HALVES):
                    last = chan_stats(0, k, h)
            stats_mean(last, 0, 0)
            dve.wait_ge(stat_mm, 1)
            link(take_mean(S[1][1]))
            stats_var(0, 0)
            dve.wait_ge(stat_mm, 2)
            take_var(S[1][1]).then_inc(var_first, 1)
            stats_scale(0, 0)
            dve.wait_ge(table_zero, 32)
            normalise(0, 0)
            dve.wait_ge(pads_clear, 7)
            for u in range(AHEAD):
                low_part(0, 0, u).then_inc(low, 1)

            def turn(i):
                for k in range(SLOTS):
                    kk, gk = k % GC, k // GC + 1
                    more = not past_end(i, k - kk + GC)
                    if kk == GC - 1 and more:
                        stats_mean(chan_stats(i, k + GC, 1), i, gk)
                    if kk < GC - 1:
                        normalise(i, k + 1)
                    for u in range(UNITS):
                        v = u + AHEAD
                        if not past_end(i, k + v // UNITS):
                            last = low_part(i, k + v // UNITS, v % UNITS)
                            if more and kk == GC - 1 and v in (MEAN_UNIT, VAR_UNIT):
                                take = take_mean if v == MEAN_UNIT else take_var
                                take(S[v % 2][1]).then_inc(low, 1)
                                wait(dve, low, 2 * UNITS, i, k, 2 * v + 2)
                                if v == MEAN_UNIT:
                                    stats_var(i, gk)
                                else:
                                    stats_scale(i, gk)
                                    normalise(i, k + 1)
                            else:
                                last.then_inc(low, 1)
                        if more and kk < GC - 1 and u in (1, 3):
                            chan_stats(i, k + GC, u // 2)
                        if more and kk == GC - 2 and u == UNITS - 1:
                            chan_stats(i, k + GC + 1, 0)
                        if u < 4:
                            final(i, k, u)

            turn(0)
            with dve.Fori(1, TURNS - 1) as i:
                turn(i)
            turn(TURNS - 1)

        @block.tensor
        def _(pe):
            def average(i, gk, var, bank):
                pe.wait_ge(vq_ready if var else mv_ready, i * 2 + (gk + 1))
                rhs, at = (SQ[:, 2, :], VAR_AT) if var else (MV[:, :, 0], MEAN_AT)
                return nc.tensor.matmul(bank[:, at:at + HALVES], avg[:, :], rhs, start=True, stop=True)

            def transposes(i, k, u, stat=None):
                if u < 4:
                    wait(pe, xn_done, 1, i, k, 1)
                elif u == 4:
                    wait(pe, b2_done, 1, i, k, 1)
                else:
                    wait(pe, b1_done, 1, i, k, 1)
                for b, (j0, j1) in enumerate(banks(u)):
                    wait(pe, low, 2 * UNITS, i, k, 2 * (u - 2) + b + 1)
                    bank = S[u % 2][b]
                    for j in range(j0, j1):
                        if u < 4:
                            src = XN[:, k % 2, u // 2, 128 * (HB * (u % 2) + j):128 * (HB * (u % 2) + j) + 128]
                        elif u == 4:
                            src = B2[:, j, :, :].rearrange("p r c -> p (r c)")
                        else:
                            src = B1[:, 128 * j:128 * j + 128]
                        op = nc.tensor.transpose(bank[:, (j - j0) * 128:(j - j0) * 128 + 128], src, ident[:, :])
                    if b == 1 and stat is not None:
                        op = average(i, stat[0], stat[1], bank)
                    op.then_inc(turned, 1)

            def products(i, k, u):
                buf = (k // GC) % 2
                if u < 4:
                    lv, width, c0 = 0, HC, HC * (u % 2)
                    hi, lo = XH[:, u // 2, :, :], XL[:, u // 2, :, :]
                    nblk = NB
                    wait(pe, low, 2 * UNITS, i, k, 2 * (u // 2 * 2 + 2))
                elif u == 4:
                    lv, width, c0, nblk, hi, lo = 2, W // 4, 0, 4, XH2, XL2
                    wait(pe, low, 2 * UNITS, i, k, 2 * u + 2)
                else:
                    lv, width, c0, nblk, hi, lo = 1, HC, 0, HB, XH1, XL1
                    wait(pe, low, 2 * UNITS, i, k, 2 * u + 2)
                m = rows_of(u)
                if u == 0:
                    wait(pe, n2q_done, 1, i, k)
                elif u == 1:
                    wait(pe, n1r_evac, 1, i, k)
                else:
                    wait(pe, fin, 4, i, k, u - 1)
                if u == 0 and k % GC == 0:
                    pe.wait_ge(tw_in[buf], (i + 1) * TWDMA)
                begun = [False, False]
                todo = []
                for j in range(nblk):
                    a0 = max(CC * j - REACH, c0)
                    a1 = min(CC * j - REACH + WIN_C, c0 + width)
                    if a1 <= a0:
                        continue
                    w0 = a0 - (CC * j - REACH)
                    for part in range(2):
                        for dy in (0, -1, 1):
                            for b, r0 in {0: ((0, 4), (1, 8)), -1: ((0, 12),), 1: ((1, 0),)}[dy]:
                                for wp in range(2 - part):
                                    todo.append((j, part, dy, b, r0, wp, a0, a1, w0))
                for n, (j, part, dy, b, r0, wp, a0, a1, w0) in enumerate(todo):
                    lhs = (lo if part else hi)[:, j, 1 + dy:1 + dy + m]
                    rhs = TW[:, buf, lv, r0:r0 + 4, w0:w0 + a1 - a0, wp, k % GC]
                    dst = O[u % 2][b][0:m, 0:4 * width].rearrange("p (r w) -> p r w", r=4)[:, :, a0 - c0:a1 - c0]
                    op = nc.tensor.matmul(dst, lhs, rhs, start=not begun[b], stop=True, skip_group_check=True)
                    begun[b] = True
                op.then_inc(mm_done, 1)

            pe.wait_ge(consts_in, 64)
            pe.wait_ge(z_ready, 1)
            for lv in range(LV):
                for q in range(4):
                    n = PATCH * PATCH
                    op = nc.tensor.transpose(S[lv // 2][lv % 2][0:n, C * q:C * q + C],
                                             ZZf[:, (4 * lv + q) * n:(4 * lv + q + 1) * n], ident[0:C, 0:C])
                op.then_inc(z_turned, 1)
            average(0, 0, False, S[1][1]).then_inc(stat_mm, 1)
            average(0, 0, True, S[1][1]).then_inc(stat_mm, 1)
            pe.wait_ge(pads_clear, 7)
            pe.wait_ge(z_low, LV)
            for u in range(AHEAD):
                transposes(0, 0, u)

            def turn(i):
                for k in range(SLOTS):
                    kk, gk = k % GC, k // GC + 1
                    more = not past_end(i, k - kk + GC)
                    for u in range(UNITS):
                        v = u + AHEAD
                        if not past_end(i, k + v // UNITS):
                            stat = (gk, v == VAR_UNIT) if more and kk == GC - 1 and v in (MEAN_UNIT, VAR_UNIT) else None
                            transposes(i, k + v // UNITS, v % UNITS, stat)
                        products(i, k, u)

            turn(0)
            with pe.Fori(1, TURNS - 1) as i:
                turn(i)
            turn(TURNS - 1)


def kernel(x, L0_conv_base_w, L0_conv_base_b, L0_conv_base_scale, L0_conv_wconv_w, L0_conv_wscale):
    import numpy as np
    import concourse.bacc as bacc
    from concourse.bass_utils import run_bass_kernel_spmd

    f32 = np.float32
    B, C, H, W = x.shape
    L = L0_conv_wconv_w.shape[0]
    PITCH, CR = 32, H // 8
    row = np.arange(128)
    pixel = row % PITCH < CR
    avg = ((row[:, None] // PITCH == row[None, :] // PITCH) & pixel[:, None] & pixel[None, :]).astype(f32) / f32(CR)
    arrays = {
        "x": np.ascontiguousarray(x),
        "base_w": np.ascontiguousarray(L0_conv_base_w[:, 0, ::-1, ::-1]),
        "base_b": np.ascontiguousarray(L0_conv_base_b),
        "base_scale": np.ascontiguousarray(L0_conv_base_scale).reshape(C),
        "wconv_w": np.ascontiguousarray(L0_conv_wconv_w[:, :, 0, ::-1, ::-1]),
        "wscale": np.ascontiguousarray(L0_conv_wscale).reshape(L, 4 * C),
        "ident": np.eye(128, dtype=f32),
        "avg": avg,
        "mask": (pixel.astype(f32) * f32(4.0)).reshape(128, 1),
    }
    nc = bacc.Bacc("TRN2", target_bir_lowering=False, num_devices=1)
    f = mybir.dt.float32
    args = [nc.dram_tensor(f"in_{n}", a.shape, f, kind="ExternalInput").ap() for n, a in arrays.items()]
    out = nc.dram_tensor("out", (B, C, H, W), f, kind="ExternalOutput").ap()
    build(nc, *args, out)
    return run_bass_kernel_spmd(nc, [{f"in_{n}": a for n, a in arrays.items()}], core_ids=[0]).results[0]["out"]
```

```python
from contextlib import ExitStack

import concourse.bass as bass
from concourse import mybir



def build(nc, x, base_w, base_b, base_scale, wconv_w, wscale, ident_c, avg_c, mask_c, out):
    f32 = mybir.dt.float32
    f16 = mybir.dt.float16
    ALU = mybir.AluOpType
    ACT = mybir.ActivationFunctionType

    B, C, H, W = x.shape
    GC = 3
    G = C // GC
    RC, CC = 8, 16
    KS = 5
    REACH = 4
    WIN_R, WIN_C = RC + 2 * REACH, CC + 2 * REACH
    PATCH = 2 * KS
    PAD_R, PAD_C = RC - 2, CC - 2
    TAB_R, TAB_C = PATCH + 2 * PAD_R, PATCH + 2 * PAD_C
    LV = 3
    S_X, S_W = 4.0, 256.0
    HALVES = 2
    IMG = B // HALVES
    PITCH = 32
    CR = H // RC
    NB = W // CC
    HB = NB // 2
    HC = W // 2
    ROW = RC * W
    UNITS = 6
    SLOTS = 6
    AHEAD = 2
    TURNS = C // SLOTS
    EPS = 1e-5
    CELL = LV * 2 * SLOTS
    Q4 = 4 * HC
    MEAN_UNIT, VAR_UNIT = 2, 3
    MEAN_AT, VAR_AT = 508, 510

    ctx = ExitStack()
    with ctx:
        def sb(name, shape, dt=f32):
            return ctx.enter_context(nc.sbuf_tensor(name, shape, dt))

        def sem(name):
            return ctx.enter_context(nc.semaphore(name))

        X = sb("X", [128, SLOTS, HALVES, ROW])
        XN = sb("XN", [128, 2, HALVES, ROW])
        RS = sb("RS", [128, ROW // 2])
        D1 = sb("D1", [128, HALVES, Q4])
        D1p = sb("D1p", [128, 2 * Q4])
        B1 = sb("B1", [128, 2 * Q4])
        RS2 = sb("RS2", [128, Q4])
        D2 = sb("D2", [128, Q4 // 2])
        D2p = sb("D2p", [64, Q4])
        B2 = sb("B2", [128, 4, RC, CC])
        XH = sb("XH", [128, HALVES, NB, 130], f16)
        XL = sb("XL", [128, HALVES, NB, 130], f16)
        XH1 = sb("XH1", [128, HB, 130], f16)
        XL1 = sb("XL1", [128, HB, 130], f16)
        XH2 = sb("XH2", [128, 4, 66], f16)
        XL2 = sb("XL2", [128, 4, 66], f16)
        TL = sb("TL", [128, WIN_R, WIN_C, LV, 2, SLOTS], f16)
        TW = sb("TW", [128, 2, LV, 2, WIN_R, WIN_C], f16)
        N2q = sb("N2q", [64, Q4])
        N2m = sb("N2m", [128, Q4 // 2])
        N1r = sb("N1r", [128, 2 * Q4])
        N1m = sb("N1m", [128, HALVES, Q4])
        ident = sb("ident", [128, 128])
        avg = sb("avg", [128, 128])
        mask = sb("mask", [128, 1])
        bias = sb("bias", [128, C])
        ST = sb("ST", [128, HALVES, GC * 4, 6])
        MV = sb("MV", [128, HALVES, 2])
        GM = sb("GM", [128, HALVES])
        SQ = sb("SQ", [128, 4, HALVES])
        RG = sb("RG", [128, HALVES])
        spare = sb("spare", [128, 1])
        ZT = sb("ZT", [PATCH * PATCH, 4, TURNS, LV, 2, SLOTS], f16)

        O = [[ctx.enter_context(nc.psum_tensor(f"O{p}{b}", [128, 512], f32)) for b in range(2)] for p in range(2)]
        S = [[ctx.enter_context(nc.psum_tensor(f"S{p}{b}", [128, 512], f32)) for b in range(2)] for p in range(2)]

        xn_flat = XN[:, :, :, :].rearrange("p a h n -> p (a h n)")
        off = [0]

        def carve(n):
            off[0] += n
            return xn_flat[0:C, off[0] - n:off[0]]

        WCf, AAf, HHf = carve(LV * 4 * 25), carve(LV * 4 * 25), carve(LV * 4 * 25)
        BWf, WSf, BSf, ZZf = carve(25), carve(LV * 4), carve(1), carve(LV * 4 * PATCH * PATCH)
        zero_n = TURNS * 4 * TAB_R * TAB_C * CELL // 128 // 2
        zeros = xn_flat[:, off[0] + 1:off[0] + 1 + zero_n // 2].bitcast(f16)

        table = nc.dram_tensor("table", [TURNS, 4, TAB_R, TAB_C, CELL], f16, kind="Internal")

        consts_in = sem("consts_in")
        weights_in = sem("weights_in")
        cleared = sem("cleared")
        zeros_ready = sem("zeros_ready")
        pads_clear = sem("pads_clear")
        table_zero = sem("table_zero")
        table_first = sem("table_first")
        table_rest = sem("table_rest")
        chain = sem("chain")
        z_ready = sem("z_ready")
        z_turned = sem("z_turned")
        z_high = sem("z_high")
        z_low = sem("z_low")
        x_in = [sem(f"x_in{s}") for s in range(SLOTS)]
        stored = [sem(f"stored{s}") for s in range(SLOTS)]
        tl_in = sem("tl_in")
        tw_done = sem("tw_done")
        mv_ready = sem("mv_ready")
        vq_ready = sem("vq_ready")
        xn_done = sem("xn_done")
        d1_done = sem("d1_done")
        rs_done = sem("rs_done")
        d1p_in = sem("d1p_in")
        b1_done = sem("b1_done")
        d2_done = sem("d2_done")
        d2p_in = sem("d2p_in")
        b2_done = sem("b2_done")
        turned = sem("turned")
        high = sem("high")
        low = sem("low")
        mm_done = sem("mm_done")
        fin = sem("fin")
        n2q_done = sem("n2q_done")
        rs2_done = sem("rs2_done")
        stat_step = sem("stat_step")
        root_done = sem("root_done")
        var_first = sem("var_first")
        stat_mm = sem("stat_mm")
        n1r_evac = sem("n1r_evac")
        n2m_in = sem("n2m_in")
        n1r_done = sem("n1r_done")
        n1m_in = sem("n1m_in")
        xadd_done = sem("xadd_done")

        block = ctx.enter_context(nc.Block())

        def wait(eng, s, per_channel, i, k, const=0):
            v = i * (per_channel * SLOTS) + (per_channel * k + const)
            if not isinstance(v, int) or v > 0:
                eng.wait_ge(s, v)

        def count(per_channel, i, k, const=0):
            return i * (per_channel * SLOTS) + (per_channel * k + const)

        XDMA = 16 * B
        TLDMA = 16 * RC * 2

        def first_of(i, k):
            return isinstance(i, int) and i == 0 and k == 0

        def past_end(i, k):
            return isinstance(i, int) and i * SLOTS + k >= C

        @block.sync
        def _(sp):
            def held(value):
                return value if isinstance(value, int) else sp.compute_val(value)

            def held_address(elements, size):
                at = held(elements)
                held(at * size)
                return at

            def wait_held(s, value):
                if not isinstance(value, int) or value > 0:
                    sp.wait_ge(s, value)

            def plane(t, b, at):
                return bass.AP(t.tensor, at + b * C * H * W, [[ROW, CR], [1, ROW]])

            def load_x(i, k):
                s = k % SLOTS
                at = held_address((i * SLOTS + k) * (H * W), 4)
                before = held(count(0, 0, 0, (i + k // SLOTS) * XDMA))
                wait_held(stored[s], before)
                for b in range(B):
                    h, bb = b // IMG, b % IMG
                    sp.dma_start(X[PITCH * bb:PITCH * bb + CR, s, h, :], plane(x, b, at)).then_inc(x_in[s], 16)

            def store_x(i, k):
                s = k % SLOTS
                at = held_address((i * SLOTS + k) * (H * W), 4)
                full = held(count(1, i, k, 1))
                wait_held(xadd_done, full)
                for b in range(B):
                    h, bb = b // IMG, b % IMG
                    sp.dma_start(plane(out, b, at), X[PITCH * bb:PITCH * bb + CR, s, h, :]).then_inc(stored[s], 16)

            def load_matrices(i, t, rows=range(RC)):
                corner = PAD_R * TAB_C * CELL
                at = held_address((i + t) * (4 * TAB_R * TAB_C * CELL) + corner, 2)
                packed = held(count(1, i + t, 0))
                wait_held(tw_done, packed)
                for r in rows:
                    for pc in range(2):
                        fixed = ((2 * (r % 2) + pc) * TAB_R - 2 * (r // 2)) * TAB_C * CELL
                        src = bass.AP(table, at + fixed, [[2 * CELL, CC // 2], [TAB_C * CELL, WIN_R],
                                                          [1, WIN_C * CELL]])
                        dst = TL[CC * r + pc:CC * r + CC:2, :, :, :, :, :]
                        sp.dma_start(dst.rearrange("p r c l a s -> p r (c l a s)"), src).then_inc(tl_in, 16)

            def d1_move(i, k):
                v, w = held(count(1, i, k, 1)), held(count(1, i, k))
                wait_held(d1_done, v)
                wait_held(b1_done, w)
                wait_held(d2_done, w)
                for h in range(HALVES):
                    sp.dma_start(D1p[64 * h:64 * h + 64, :], D1[:, h, :]).then_inc(d1p_in, 16)

            def d2_move(i, k):
                v, w = held(count(1, i, k, 1)), held(count(1, i, k))
                wait_held(d2_done, v)
                wait_held(b2_done, w)
                sp.dma_start(D2p[:, :], D2[:, :]).then_inc(d2p_in, 16)

            def n2_move(i, k):
                v, w = held(count(1, i, k, 1)), held(count(1, i, k))
                wait_held(n2q_done, v)
                wait_held(n1r_done, w)
                sp.dma_start(N2m[:, :], N2q[:, :]).then_inc(n2m_in, 16)

            def n1_move(i, k):
                v, w = held(count(1, i, k, 1)), held(count(1, i, k))
                wait_held(n1r_done, v)
                wait_held(xadd_done, w)
                for h in range(HALVES):
                    sp.dma_start(N1m[:, h, :], N1r[64 * h:64 * h + 64, :]).then_inc(n1m_in, 16)

            sp.dma_start(WCf.rearrange("c (l n) -> c l n", l=LV),
                         wconv_w.rearrange("l (c s) a b -> c l (s a b)", s=4)).then_inc(weights_in, 16)
            sp.dma_start(BWf, base_w.rearrange("c a b -> c (a b)")).then_inc(weights_in, 16)
            sp.dma_start(WSf.rearrange("c (l n) -> c l n", l=LV),
                         wscale.rearrange("l (c s) -> c l s", s=4)).then_inc(weights_in, 16)
            sp.dma_start(BSf, base_scale.rearrange("(c o) -> c o", o=1)).then_inc(weights_in, 16)
            sp.dma_start(ident[:, :], ident_c).then_inc(consts_in, 16)
            sp.dma_start(avg[:, :], avg_c).then_inc(consts_in, 16)
            sp.dma_start(mask[:, :], mask_c).then_inc(consts_in, 16)
            sp.dma_start(bias[:, :], base_b.partition_broadcast(128)).then_inc(consts_in, 16)
            sp.wait_ge(cleared, 3)
            for k in range(GC):
                load_x(0, k)
            flat = table.ap().rearrange("g q r c n -> (g q r c n)").rearrange("(a p n) -> a p n", a=2, p=128)
            sp.wait_ge(zeros_ready, 1)
            for a in range(2):
                sp.dma_start(flat[a], zeros).then_inc(table_zero, 16)
            load_x(0, GC)
            sp.wait_ge(table_zero, 32)
            sp.wait_ge(z_low, LV)
            def write_table(turns, s):
                for t in turns:
                    for q in range(4):
                        stored_q = 2 * (q // 2) + 1 - q % 2
                        dst = table.ap()[t, stored_q, PAD_R:PAD_R + PATCH, PAD_C:PAD_C + PATCH, :]
                        sp.dma_start(dst, ZT[:, q, t, :, :, :].rearrange("p l a s -> p (l a s)")).then_inc(s, 16)

            write_table([0], table_first)
            sp.wait_ge(table_first, 16 * 4)
            load_matrices(0, 0)
            d1_move(0, 0)
            d2_move(0, 0)

            def turn(i):
                for k in range(SLOTS):
                    if not first_of(i, k):
                        n1_move(i, k - 1)
                    if not past_end(i, k + 4):
                        load_x(i, k + 4)
                    if not past_end(i, k + 1):
                        d1_move(i, k + 1)
                    matrices = k == SLOTS - 2 and not past_end(i + 1, 0)
                    if matrices:
                        sp.wait_ge(table_rest, 16 * 4 * (TURNS - 1))
                        load_matrices(i, 1, range(0, RC // 2))
                    n2_move(i, k)
                    if not past_end(i, k + 1):
                        d2_move(i, k + 1)
                    if matrices:
                        load_matrices(i, 1, range(RC // 2, RC))
                    if not first_of(i, k):
                        store_x(i, k - 1)
                    if isinstance(i, int) and i == 0 and 0 < k < 4:
                        write_table(range(1 + 5 * (k - 1), 1 + 5 * k), table_rest)

            turn(0)
            with sp.Fori(1, TURNS - 1) as i:
                turn(i)
            turn(TURNS - 1)
            n1_move(TURNS, -1)
            store_x(TURNS, -1)
            for s in range(SLOTS):
                sp.wait_ge(stored[s], TURNS * XDMA)

        @block.gpsimd
        def _(pool):
            nc.gpsimd.memset(X[:, 4:6, :, :], 0.0).then_inc(cleared, 1)

            def d1_sum(i, k):
                wait(pool, xn_done, 1, i, k, 1)
                wait(pool, d1p_in, 32, i, k)
                for h in range(HALVES):
                    if h == 0:
                        wait(pool, d1_done, 1, i, k)
                    else:
                        wait(pool, rs_done, 3, i, k, 2)
                    v = XN[:, k % 2, h, :].rearrange("p (jr two c) -> p jr two c", two=2, c=CC)
                    nc.gpsimd.tensor_tensor(RS[:, :].rearrange("p (jr c) -> p jr c", c=CC), v[:, :, 0, :],
                                            v[:, :, 1, :], ALU.add).then_inc(rs_done, 1)
                    wait(pool, rs_done, 3, i, k, 2 * h + 1)
                    t = RS[:, :].rearrange("p (j r q two) -> p r j q two", j=NB, r=4, two=2)
                    o = D1[:, h, :].rearrange("p (r j q) -> p r j q", r=4, q=CC // 2)[:, :, :, ::-1]
                    nc.gpsimd.tensor_tensor(o, t[:, :, :, :, 0], t[:, :, :, :, 1],
                                            ALU.add).then_inc(d1_done if h else rs_done, 1)

            def d2_sum(i, k):
                wait(pool, d1p_in, 32, i, k, 32)
                wait(pool, d2p_in, 16, i, k)
                v = D1p[:, :].rearrange("p (r two c) -> p r two c", two=2, c=HC)
                nc.gpsimd.tensor_tensor(RS2[:, :].rearrange("p (r c) -> p r c", r=4), v[:, :, 0, :], v[:, :, 1, :],
                                        ALU.add).then_inc(rs2_done, 1)
                wait(pool, rs2_done, 1, i, k, 1)
                t = RS2[:, :].rearrange("p (n two) -> p n two", two=2)
                nc.gpsimd.tensor_tensor(D2[:, :], t[:, :, 0], t[:, :, 1], ALU.add).then_inc(d2_done, 1)

            def up(v, cols):
                return v.rearrange("p (r c o) -> p r c o", r=4, o=1).to_broadcast([128, 4, cols, 2])

            def n1_add(i, k):
                wait(pool, n2m_in, 16, i, k, 16)
                wait(pool, n1r_evac, 1, i, k, 1)
                v = N1r[:, :].rearrange("p (r two c d) -> p r two c d", two=2, c=HC // 2, d=2)
                for a in range(2):
                    op = nc.gpsimd.tensor_tensor(v[:, :, a, :, :], v[:, :, a, :, :], up(N2m[:, :], HC // 2), ALU.add)
                op.then_inc(n1r_done, 1)

            def x_add(i, k):
                wait(pool, n1m_in, 32, i, k, 32)
                wait(pool, fin, 4, i, k, 4)
                for h in range(HALVES):
                    v = X[:, k % SLOTS, h, :].rearrange("p (r two c d) -> p r two c d", two=2, c=HC, d=2)
                    for a in range(2):
                        op = nc.gpsimd.tensor_tensor(v[:, :, a, :, :], v[:, :, a, :, :], up(N1m[:, h, :], HC), ALU.add)
                op.then_inc(xadd_done, 1)

            d1_sum(0, 0)
            d2_sum(0, 0)

            def turn(i):
                for k in range(SLOTS):
                    if not first_of(i, k):
                        n1_add(i, k - 1)
                    if not past_end(i, k + 1):
                        d1_sum(i, k + 1)
                    if not first_of(i, k):
                        x_add(i, k - 1)
                    if not past_end(i, k + 1):
                        d2_sum(i, k + 1)

            turn(0)
            with pool.Fori(1, TURNS - 1) as i:
                turn(i)
            turn(TURNS - 1)
            n1_add(TURNS, -1)
            x_add(TURNS, -1)

        def split_dst(u, hi):
            if u < 4:
                h, c = u // 2, u % 2
                return (XH if hi else XL)[:, h, HB * c:HB * c + HB, 1:129]
            if u == 4:
                return (XH2 if hi else XL2)[:, :, 1:65]
            return (XH1 if hi else XL1)[:, :, 1:129]

        def banks(u):
            return [(0, 2), (2, 4)] if u == 4 else [(0, 4), (4, 7)]

        def rows_of(u):
            return 64 if u == 4 else 128

        def split_wait(eng, u, i, k):
            last = (2, 2, 4, 4, 5, 6)[u] - UNITS
            wait(eng, mm_done, UNITS, i, k, last)

        @block.scalar
        def _(act):
            nc.scalar.memzero(X[:, 2:4, :, :]).then_inc(cleared, 1)
            for lv in range(LV):
                act.wait_ge(z_turned, lv + 1)
                src = S[lv // 2][lv % 2][0:PATCH * PATCH, 0:4 * C].rearrange("p (t s) -> p t s", s=SLOTS)
                dst = ZT[:, :, :, lv, 0, :].rearrange("p q t s -> p (q t) s")
                nc.scalar.activation(dst, src, ACT.Copy).then_inc(z_high, 1)

            def high_part(i, k, u):
                split_wait(act, u, i, k)
                for b, (j0, j1) in enumerate(banks(u)):
                    wait(act, turned, 2 * UNITS, i, k, 2 * u + b + 1)
                    src = S[u % 2][b][:, 0:(j1 - j0) * 128].rearrange("p (j m) -> p j m", m=128)[:, :, 0:rows_of(u)]
                    nc.scalar.activation(split_dst(u, True)[:, j0:j1, :], src, ACT.Copy).then_inc(high, 1)

            def pack(i, k, lv):
                if lv == 0:
                    act.wait_ge(tl_in, (i + k // SLOTS + 1) * TLDMA)
                    wait(act, mm_done, UNITS, i, k - 1)
                src = TL[:, :, :, lv, :, k % SLOTS].rearrange("p r c a -> p a (r c)")
                dst = TW[:, k % 2, lv, :, :, :].rearrange("p a r c -> p a (r c)")
                op = nc.scalar.activation(dst, src, ACT.Copy)
                if lv == LV - 1:
                    op.then_inc(tw_done, 1)

            def b1_copy(i, k):
                wait(act, d1p_in, 32, i, k, 32)
                wait(act, turned, 2 * UNITS, i, k - 1, 2 * UNITS)
                src = D1p[:, :].rearrange("p (r j c) -> p r j c", r=RC, c=CC)
                dst = B1[:, :].rearrange("p (j r c) -> p r j c", r=RC, c=CC)[:, :, :, ::-1]
                nc.scalar.activation(dst, src, ACT.Copy).then_inc(b1_done, 1)

            def b2_copy(i, k):
                wait(act, d2p_in, 16, i, k, 16)
                wait(act, turned, 2 * UNITS, i, k - 1, 2 * UNITS - 2)
                v = D2p[:, :].rearrange("p (r c) -> p r c", r=RC)
                src = v[:, :, 0:48].rearrange("p r (j c) -> p r j c", c=CC)
                dst = B2[0:64, 0:3, :, :].rearrange("p j r c -> p r j c")[:, :, :, ::-1]
                nc.scalar.activation(dst, src, ACT.Copy)
                nc.scalar.activation(B2[0:64, 3, :, 8:16][:, :, ::-1], v[:, :, 48:56], ACT.Copy).then_inc(b2_done, 1)

            def n2_evac(i, k):
                wait(act, mm_done, UNITS, i, k, 5)
                wait(act, n2m_in, 16, i, k)
                for b in range(2):
                    op = nc.scalar.activation(N2q[:, b * 224:b * 224 + 224], O[0][b][0:64, 0:224], ACT.Copy,
                                              scale=0.25 / (4 * S_X * S_W))
                op.then_inc(n2q_done, 1)

            def n1_evac(i, k):
                wait(act, mm_done, UNITS, i, k, 6)
                wait(act, n1m_in, 32, i, k)
                for b in range(2):
                    op = nc.scalar.activation(N1r[:, b * Q4:b * Q4 + Q4], O[1][b][:, 0:Q4], ACT.Identity,
                                              scale=0.5 / (2 * S_X * S_W), bias=bias[:, bass.ds(i * SLOTS + k, 1)])
                op.then_inc(n1r_evac, 1)

            def root():
                nc.scalar.activation(SQ[:, 1, :], SQ[:, 0, :], ACT.Sqrt).then_inc(root_done, 1)

            act.wait_ge(var_first, 1)
            root()
            act.wait_ge(pads_clear, 7)
            act.wait_ge(consts_in, 64)
            for u in range(AHEAD):
                high_part(0, 0, u)
            for lv in range(LV):
                pack(0, 0, lv)

            def turn(i):
                for k in range(SLOTS):
                    for u in range(UNITS):
                        v = u + AHEAD
                        if not past_end(i, k + v // UNITS):
                            high_part(i, k + v // UNITS, v % UNITS)
                        if v == VAR_UNIT and k % GC == GC - 1 and not past_end(i, k + 1):
                            wait(act, low, 2 * UNITS, i, k, 2 * v + 2)
                            root()
                        if k < SLOTS - 1 and u < LV:
                            pack(i, k + 1, u)
                        if k == SLOTS - 1 and u >= UNITS - LV and not past_end(i, k + 1):
                            pack(i, k + 1, u - (UNITS - LV))
                        if u == 0:
                            b2_copy(i, k)
                        if u == 1:
                            b1_copy(i, k)
                        if u == 4:
                            n2_evac(i, k)
                    n1_evac(i, k)

            turn(0)
            with act.Fori(1, TURNS - 1) as i:
                turn(i)
            turn(TURNS - 1)

        @block.vector
        def _(dve):
            links = [0]

            def link(op):
                links[0] += 1
                op.then_inc(chain, 1)
                dve.wait_ge(chain, links[0])

            nc.vector.memset(X[:, 0:2, :, :], 0.0).then_inc(cleared, 1)
            nc.vector.memset(zeros, 0.0).then_inc(zeros_ready, 1)
            for t in (XH, XL):
                nc.vector.memset(t[:, :, :, :], 0.0).then_inc(pads_clear, 1)
            for t in (XH1, XL1, XH2, XL2):
                nc.vector.memset(t[:, :, :], 0.0).then_inc(pads_clear, 1)
            nc.vector.memset(B2[:, :, :, :], 0.0).then_inc(pads_clear, 1)

            dve.wait_ge(weights_in, 64)
            WC = WCf.rearrange("c (ls n) -> c ls n", n=25)
            link(nc.vector.tensor_tensor(WC, WC, WSf.rearrange("c (ls o) -> c ls o", o=1)
                                         .to_broadcast([C, LV * 4, 25]), ALU.mult))
            W4 = WCf.rearrange("c (lp two n) -> c lp two n", two=2, n=25)
            A4 = AAf.rearrange("c (lp two n) -> c lp two n", two=2, n=25)
            link(nc.vector.tensor_tensor(A4[:, :, 0, :], W4[:, :, 0, :], W4[:, :, 1, :], ALU.add))
            link(nc.vector.tensor_tensor(A4[:, :, 1, :], W4[:, :, 0, :], W4[:, :, 1, :], ALU.subtract))
            A2 = AAf.rearrange("c (l two n) -> c l two n", l=LV, two=2)
            H2 = HHf.rearrange("c (l two n) -> c l two n", l=LV, two=2)
            link(nc.vector.tensor_tensor(H2[:, :, 0, :], A2[:, :, 0, :], A2[:, :, 1, :], ALU.add))
            link(nc.vector.tensor_tensor(H2[:, :, 1, :], A2[:, :, 0, :], A2[:, :, 1, :], ALU.subtract))
            HV = HHf.rearrange("c (l x a b) -> c l x a b", l=LV, x=4, a=KS)
            Z = ZZf.rearrange("c (l q a b) -> c l q a b", l=LV, q=4, a=PATCH)
            for q in range(4):
                for o in range(4):
                    link(nc.vector.tensor_scalar(Z[:, :, q, o // 2::2, o % 2::2], HV[:, :, q ^ o, :, :],
                                                 0.25 * S_W, None, ALU.mult))
            BW = BWf.rearrange("c (a b) -> c a b", a=KS)
            link(nc.vector.tensor_scalar(BWf, BWf, BSf, S_W, ALU.mult, ALU.mult))
            for q in range(4):
                t = Z[:, 0, q, q // 2 + 2:q // 2 + 2 + KS, q % 2 + 2:q % 2 + 2 + KS]
                op = nc.vector.tensor_tensor(t, t, BW, ALU.add)
                if q == 3:
                    op.then_inc(z_ready, 1)
                else:
                    link(op)
            for lv in range(LV):
                dve.wait_ge(z_high, lv + 1)
                src = S[lv // 2][lv % 2][0:PATCH * PATCH, 0:4 * C].rearrange("p (t s) -> p t s", s=SLOTS)
                z = ZT[:, :, :, lv, :, :].rearrange("p q t a s -> p (q t) a s")
                nc.vector.tensor_tensor(z[:, :, 1, :], src, z[:, :, 0, :], ALU.subtract).then_inc(z_low, 1)

            def chan_stats(i, k, h):
                dve.wait_ge(x_in[k % SLOTS], (i + k // SLOTS + 1) * XDMA)
                for c in range(4):
                    op = nc.vector.bn_stats(ST[:, h, 4 * (k % GC) + c, :], X[:, k % SLOTS, h, c * Q4:(c + 1) * Q4])
                return op

            STEPS = 8

            def step(op, i, gk, n):
                op.then_inc(stat_step, 1)
                dve.wait_ge(stat_step, i * (2 * STEPS) + (gk * STEPS + n))

            def stats_mean(last, i, gk):
                step(last, i, gk, 1)
                nc.vector.memset(spare[:, :], 0.0)
                for h in range(HALVES):
                    op = nc.vector.bn_aggr(MV[:, h, :], ST[:, h, :, :].rearrange("p a b -> p (a b)"))
                op.then_inc(mv_ready, 1)

            def take_mean(bank):
                return nc.vector.tensor_copy(GM[:, :], bank[:, MEAN_AT:MEAN_AT + HALVES])

            def stats_var(i, gk):
                step(nc.vector.tensor_tensor(SQ[:, 0, :], MV[:, :, 0], GM[:, :], ALU.subtract), i, gk, 2)
                step(nc.vector.tensor_tensor(SQ[:, 1, :], SQ[:, 0, :], SQ[:, 0, :], ALU.mult), i, gk, 3)
                nc.vector.tensor_tensor(SQ[:, 2, :], SQ[:, 1, :], MV[:, :, 1], ALU.add).then_inc(vq_ready, 1)

            def take_var(bank):
                return nc.vector.tensor_scalar(SQ[:, 0, :], bank[:, VAR_AT:VAR_AT + HALVES], EPS, None, ALU.add)

            def stats_scale(i, gk):
                dve.wait_ge(root_done, i * 2 + (gk + 1))
                step(nc.vector.reciprocal(SQ[:, 1, :], SQ[:, 1, :]), i, gk, 4)
                step(nc.vector.tensor_tensor(SQ[:, 3, :], SQ[:, 1, :], SQ[:, 1, :], ALU.mult), i, gk, 5)
                step(nc.vector.tensor_tensor(SQ[:, 3, :], SQ[:, 3, :], SQ[:, 0, :], ALU.mult), i, gk, 6)
                step(nc.vector.tensor_scalar(SQ[:, 3, :], SQ[:, 3, :], -0.5, 1.5, ALU.mult, ALU.add), i, gk, 7)
                step(nc.vector.scalar_tensor_tensor(RG[:, :], SQ[:, 1, :], mask[:, 0:1], SQ[:, 3, :], ALU.mult,
                                                    ALU.mult), i, gk, 8)

            def normalise(i, k):
                wait(dve, turned, 2 * UNITS, i, k - 2, 8)
                wait(dve, d1_done, 1, i, k - 1)
                for h in range(HALVES):
                    src = X[:, k % SLOTS, h, :].rearrange("p (r j c) -> p r j c", r=RC, c=CC)
                    dst = XN[:, k % 2, h, :].rearrange("p (j r c) -> p r j c", r=RC, c=CC)[:, :, :, ::-1]
                    op = nc.vector.tensor_scalar(dst, src, GM[:, h:h + 1], RG[:, h:h + 1], ALU.subtract, ALU.mult)
                op.then_inc(xn_done, 1)

            def low_part(i, k, u):
                for b, (j0, j1) in enumerate(banks(u)):
                    wait(dve, high, 2 * UNITS, i, k, 2 * u + b + 1)
                    src = S[u % 2][b][:, 0:(j1 - j0) * 128].rearrange("p (j m) -> p j m", m=128)[:, :, 0:rows_of(u)]
                    op = nc.vector.tensor_tensor(split_dst(u, False)[:, j0:j1, :], src,
                                                 split_dst(u, True)[:, j0:j1, :], ALU.subtract)
                    if b == 0:
                        op.then_inc(low, 1)
                return op

            def final(i, k, u):
                wait(dve, mm_done, UNITS, i, k, u + 1)
                h, c = u // 2, u % 2
                for b in range(2):
                    t = X[:, k % SLOTS, h, :].rearrange("p (b r w) -> p b r w", b=2, r=4)[:, b, :, HC * c:HC * c + HC]
                    op = nc.vector.scalar_tensor_tensor(t, O[u % 2][b][:, 0:Q4].rearrange("p (r w) -> p r w", r=4),
                                                        1.0 / (S_X * S_W), t, ALU.mult, ALU.add)
                op.then_inc(fin, 1)

            dve.wait_ge(consts_in, 64)
            for k in range(GC):
                for h in range(HALVES):
                    last = chan_stats(0, k, h)
            stats_mean(last, 0, 0)
            dve.wait_ge(stat_mm, 1)
            link(take_mean(S[1][1]))
            stats_var(0, 0)
            dve.wait_ge(stat_mm, 2)
            take_var(S[1][1]).then_inc(var_first, 1)
            stats_scale(0, 0)
            dve.wait_ge(table_zero, 32)
            normalise(0, 0)
            dve.wait_ge(pads_clear, 7)
            for u in range(AHEAD):
                low_part(0, 0, u).then_inc(low, 1)

            def turn(i):
                for k in range(SLOTS):
                    kk, gk = k % GC, k // GC + 1
                    more = not past_end(i, k - kk + GC)
                    if kk == GC - 1 and more:
                        stats_mean(last_stats, i, gk)
                    if kk < GC - 1:
                        normalise(i, k + 1)
                    for u in range(UNITS):
                        v = u + AHEAD
                        if not past_end(i, k + v // UNITS):
                            last = low_part(i, k + v // UNITS, v % UNITS)
                            if more and kk == GC - 1 and v in (MEAN_UNIT, VAR_UNIT):
                                take = take_mean if v == MEAN_UNIT else take_var
                                take(S[v % 2][1]).then_inc(low, 1)
                                wait(dve, low, 2 * UNITS, i, k, 2 * v + 2)
                                if v == MEAN_UNIT:
                                    stats_var(i, gk)
                                else:
                                    stats_scale(i, gk)
                                    normalise(i, k + 1)
                            else:
                                last.then_inc(low, 1)
                        if more and kk < GC - 1 and u in (1, 3):
                            chan_stats(i, k + GC, u // 2)
                        if more and kk == GC - 2 and u >= UNITS - 2:
                            last_stats = chan_stats(i, k + GC + 1, u - (UNITS - 2))
                        if u < 4:
                            final(i, k, u)

            turn(0)
            with dve.Fori(1, TURNS - 1) as i:
                turn(i)
            turn(TURNS - 1)

        @block.tensor
        def _(pe):
            def average(i, gk, var, bank):
                pe.wait_ge(vq_ready if var else mv_ready, i * 2 + (gk + 1))
                rhs, at = (SQ[:, 2, :], VAR_AT) if var else (MV[:, :, 0], MEAN_AT)
                return nc.tensor.matmul(bank[:, at:at + HALVES], avg[:, :], rhs, start=True, stop=True)

            def transposes(i, k, u, stat=None):
                if u < 4:
                    wait(pe, xn_done, 1, i, k, 1)
                elif u == 4:
                    wait(pe, b2_done, 1, i, k, 1)
                else:
                    wait(pe, b1_done, 1, i, k, 1)
                for b, (j0, j1) in enumerate(banks(u)):
                    wait(pe, low, 2 * UNITS, i, k, 2 * (u - 2) + b + 1)
                    bank = S[u % 2][b]
                    for j in range(j0, j1):
                        if u < 4:
                            src = XN[:, k % 2, u // 2, 128 * (HB * (u % 2) + j):128 * (HB * (u % 2) + j) + 128]
                        elif u == 4:
                            src = B2[:, j, :, :].rearrange("p r c -> p (r c)")
                        else:
                            src = B1[:, 128 * j:128 * j + 128]
                        op = nc.tensor.transpose(bank[:, (j - j0) * 128:(j - j0) * 128 + 128], src, ident[:, :])
                    if b == 1 and stat is not None:
                        op = average(i, stat[0], stat[1], bank)
                    op.then_inc(turned, 1)

            def products(i, k, u):
                if u < 4:
                    lv, width, c0 = 0, HC, HC * (u % 2)
                    hi, lo = XH[:, u // 2, :, :], XL[:, u // 2, :, :]
                    nblk = NB
                    wait(pe, low, 2 * UNITS, i, k, 2 * (u // 2 * 2 + 2))
                elif u == 4:
                    lv, width, c0, nblk, hi, lo = 2, W // 4, 0, 4, XH2, XL2
                    wait(pe, low, 2 * UNITS, i, k, 2 * u + 2)
                else:
                    lv, width, c0, nblk, hi, lo = 1, HC, 0, HB, XH1, XL1
                    wait(pe, low, 2 * UNITS, i, k, 2 * u + 2)
                m = rows_of(u)
                if u == 0:
                    wait(pe, n2q_done, 1, i, k)
                elif u == 1:
                    wait(pe, n1r_evac, 1, i, k)
                else:
                    wait(pe, fin, 4, i, k, u - 1)
                if u == 0:
                    wait(pe, tw_done, 1, i, k, 1)
                begun = [False, False]
                def product(j, part, wp, dy, b, r0, rows):
                    a0 = max(CC * j - REACH, c0)
                    a1 = min(CC * j - REACH + WIN_C, c0 + width)
                    if a1 <= a0:
                        return None
                    w0 = a0 - (CC * j - REACH)
                    lhs = (lo if part else hi)[rows, j, 1 + dy:1 + dy + m]
                    rhs = TW[rows, k % 2, lv, wp, r0:r0 + 4, w0:w0 + a1 - a0]
                    dst = O[u % 2][b][0:m, 0:4 * width].rearrange("p (r w) -> p r w", r=4)[:, :, a0 - c0:a1 - c0]
                    op = nc.tensor.matmul(dst, lhs, rhs, start=not begun[b], stop=True, skip_group_check=True)
                    begun[b] = True
                    return op

                every = slice(0, 128)
                top, bottom = (slice(0, 64), slice(64, 128)) if m == 128 else (every, every)
                op = None
                for j in range(nblk):
                    for part in range(2):
                        for b, r0 in ((0, 4), (1, 8)):
                            for wp in range(2 - part):
                                op = product(j, part, wp, 0, b, r0, every) or op
                for j in range(nblk):
                    for part in range(2):
                        for wp in range(2 - part):
                            op = product(j, part, wp, -1, 0, 12, bottom) or op
                            op = product(j, part, wp, 1, 1, 0, top) or op
                op.then_inc(mm_done, 1)

            pe.wait_ge(consts_in, 64)
            pe.wait_ge(z_ready, 1)
            for lv in range(LV):
                for q in range(4):
                    n = PATCH * PATCH
                    op = nc.tensor.transpose(S[lv // 2][lv % 2][0:n, C * q:C * q + C],
                                             ZZf[:, (4 * lv + q) * n:(4 * lv + q + 1) * n], ident[0:C, 0:C])
                op.then_inc(z_turned, 1)
            average(0, 0, False, S[1][1]).then_inc(stat_mm, 1)
            average(0, 0, True, S[1][1]).then_inc(stat_mm, 1)
            pe.wait_ge(pads_clear, 7)
            pe.wait_ge(z_low, LV)
            for u in range(AHEAD):
                transposes(0, 0, u)

            def turn(i):
                for k in range(SLOTS):
                    kk, gk = k % GC, k // GC + 1
                    more = not past_end(i, k - kk + GC)
                    for u in range(UNITS):
                        v = u + AHEAD
                        if not past_end(i, k + v // UNITS):
                            stat = (gk, v == VAR_UNIT) if more and kk == GC - 1 and v in (MEAN_UNIT, VAR_UNIT) else None
                            transposes(i, k + v // UNITS, v % UNITS, stat)
                        products(i, k, u)

            turn(0)
            with pe.Fori(1, TURNS - 1) as i:
                turn(i)
            turn(TURNS - 1)


def kernel(x, L0_conv_base_w, L0_conv_base_b, L0_conv_base_scale, L0_conv_wconv_w, L0_conv_wscale):
    import numpy as np
    import concourse.bacc as bacc
    from concourse.bass_utils import run_bass_kernel_spmd

    f32 = np.float32
    B, C, H, W = x.shape
    L = L0_conv_wconv_w.shape[0]
    PITCH, CR = 32, H // 8
    row = np.arange(128)
    pixel = row % PITCH < CR
    avg = ((row[:, None] // PITCH == row[None, :] // PITCH) & pixel[:, None] & pixel[None, :]).astype(f32) / f32(CR)
    arrays = {
        "x": np.ascontiguousarray(x),
        "base_w": np.ascontiguousarray(L0_conv_base_w[:, 0, ::-1, ::-1]),
        "base_b": np.ascontiguousarray(L0_conv_base_b),
        "base_scale": np.ascontiguousarray(L0_conv_base_scale).reshape(C),
        "wconv_w": np.ascontiguousarray(L0_conv_wconv_w[:, :, 0, ::-1, ::-1]),
        "wscale": np.ascontiguousarray(L0_conv_wscale).reshape(L, 4 * C),
        "ident": np.eye(128, dtype=f32),
        "avg": avg,
        "mask": (pixel.astype(f32) * f32(4.0)).reshape(128, 1),
    }
    nc = bacc.Bacc("TRN2", target_bir_lowering=False, num_devices=1)
    f = mybir.dt.float32
    args = [nc.dram_tensor(f"in_{n}", a.shape, f, kind="ExternalInput").ap() for n, a in arrays.items()]
    out = nc.dram_tensor("out", (B, C, H, W), f, kind="ExternalOutput").ap()
    build(nc, *args, out)
    return run_bass_kernel_spmd(nc, [{f"in_{n}": a for n, a in arrays.items()}], core_ids=[0]).results[0]["out"]
```

```python
from contextlib import ExitStack

import concourse.bass as bass
from concourse import mybir



def build(nc, x, base_w, base_b, base_scale, wconv_w, wscale, ident_c, avg_c, mask_c, out):
    f32 = mybir.dt.float32
    f16 = mybir.dt.float16
    ALU = mybir.AluOpType
    ACT = mybir.ActivationFunctionType

    B, C, H, W = x.shape
    GC = 3
    G = C // GC
    RC, CC = 8, 16
    KS = 5
    REACH = 4
    WIN_R, WIN_C = RC + 2 * REACH, CC + 2 * REACH
    PATCH = 2 * KS
    PAD_R, PAD_C = RC - 2, CC - 2
    TAB_R, TAB_C = PATCH + 2 * PAD_R, PATCH + 2 * PAD_C
    LV = 3
    S_X, S_W = 4.0, 256.0
    HALVES = 2
    IMG = B // HALVES
    PITCH = 32
    CR = H // RC
    NB = W // CC
    HB = NB // 2
    HC = W // 2
    ROW = RC * W
    UNITS = 6
    SLOTS = 6
    AHEAD = 2
    TURNS = C // SLOTS
    EPS = 1e-5
    CELL = LV * 2 * SLOTS
    Q4 = 4 * HC
    MEAN_UNIT, VAR_UNIT = 2, 3
    MEAN_AT, VAR_AT = 508, 510

    ctx = ExitStack()
    with ctx:
        def sb(name, shape, dt=f32):
            return ctx.enter_context(nc.sbuf_tensor(name, shape, dt))

        def sem(name):
            return ctx.enter_context(nc.semaphore(name))

        X = sb("X", [128, SLOTS, HALVES, ROW])
        XN = sb("XN", [128, 2, HALVES, ROW])
        RS = sb("RS", [128, ROW // 2])
        D1 = sb("D1", [128, HALVES, Q4])
        D1p = sb("D1p", [128, 2 * Q4])
        B1 = sb("B1", [128, 2 * Q4])
        RS2 = sb("RS2", [128, Q4])
        D2 = sb("D2", [128, Q4 // 2])
        D2p = sb("D2p", [64, Q4])
        B2 = sb("B2", [128, 4, RC, CC])
        XH = sb("XH", [128, HALVES, NB, 130], f16)
        XL = sb("XL", [128, HALVES, NB, 130], f16)
        XH1 = sb("XH1", [128, HB, 130], f16)
        XL1 = sb("XL1", [128, HB, 130], f16)
        XH2 = sb("XH2", [128, 4, 66], f16)
        XL2 = sb("XL2", [128, 4, 66], f16)
        TL = sb("TL", [128, WIN_R, WIN_C, LV, 2, SLOTS], f16)
        TW = sb("TW", [128, 2, LV, 2, WIN_R, WIN_C], f16)
        N2q = sb("N2q", [64, Q4])
        N2m = sb("N2m", [128, Q4 // 2])
        N1r = sb("N1r", [128, 2 * Q4])
        N1m = sb("N1m", [128, HALVES, Q4])
        ident = sb("ident", [128, 128])
        avg = sb("avg", [128, 128])
        mask = sb("mask", [128, 1])
        bias = sb("bias", [128, C])
        ST = sb("ST", [128, HALVES, GC * 4, 6])
        MV = sb("MV", [128, HALVES, 2])
        GM = sb("GM", [128, HALVES])
        SQ = sb("SQ", [128, 4, HALVES])
        RG = sb("RG", [128, HALVES])
        spare = sb("spare", [128, 1])
        ZT = sb("ZT", [PATCH * PATCH, 4, TURNS, LV, 2, SLOTS], f16)

        O = [[ctx.enter_context(nc.psum_tensor(f"O{p}{b}", [128, 512], f32)) for b in range(2)] for p in range(2)]
        S = [[ctx.enter_context(nc.psum_tensor(f"S{p}{b}", [128, 512], f32)) for b in range(2)] for p in range(2)]

        xn_flat = XN[:, :, :, :].rearrange("p a h n -> p (a h n)")
        off = [0]

        def carve(n):
            off[0] += n
            return xn_flat[0:C, off[0] - n:off[0]]

        WCf, AAf, HHf = carve(LV * 4 * 25), carve(LV * 4 * 25), carve(LV * 4 * 25)
        BWf, WSf, BSf, ZZf = carve(25), carve(LV * 4), carve(1), carve(LV * 4 * PATCH * PATCH)
        ZP, ZPIECES = 96, 3
        zeros = X[0:ZP, SLOTS - 1, :, :].rearrange("p h n -> p (h n)").bitcast(f16)
        zero_first = 4 * TAB_R * TAB_C * CELL // ZP
        zero_rest = (TURNS - 1) * zero_first // ZPIECES

        table = nc.dram_tensor("table", [TURNS, 4, TAB_R, TAB_C, CELL], f16, kind="Internal")

        consts_in = sem("consts_in")
        weights_in = sem("weights_in")
        x_clear = [sem(f"x_clear{s}") for s in range(SLOTS)]
        pads_clear = sem("pads_clear")
        zero_first_in = sem("zero_first_in")
        zero_rest_in = sem("zero_rest_in")
        table_first = sem("table_first")
        table_second = sem("table_second")
        table_rest = sem("table_rest")
        chain = sem("chain")
        z_ready = sem("z_ready")
        z_turned = sem("z_turned")
        z_high = sem("z_high")
        z_low = sem("z_low")
        x_in = [sem(f"x_in{s}") for s in range(SLOTS)]
        stored = [sem(f"stored{s}") for s in range(SLOTS)]
        tl_in = sem("tl_in")
        tw_done = sem("tw_done")
        mv_ready = sem("mv_ready")
        vq_ready = sem("vq_ready")
        xn_done = sem("xn_done")
        d1_done = sem("d1_done")
        rs_done = sem("rs_done")
        d1p_in = sem("d1p_in")
        b1_done = sem("b1_done")
        d2_done = sem("d2_done")
        d2p_in = sem("d2p_in")
        b2_done = sem("b2_done")
        turned = sem("turned")
        high = sem("high")
        low = sem("low")
        mm_done = sem("mm_done")
        round_done = sem("round_done")
        fin = sem("fin")
        n2q_done = sem("n2q_done")
        rs2_done = sem("rs2_done")
        stat_step = sem("stat_step")
        root_done = sem("root_done")
        var_first = sem("var_first")
        stat_mm = sem("stat_mm")
        n1r_evac = sem("n1r_evac")
        n2m_in = sem("n2m_in")
        n1r_done = sem("n1r_done")
        n1m_in = sem("n1m_in")
        xadd_done = sem("xadd_done")
        last_half = sem("last_half")

        block = ctx.enter_context(nc.Block())

        def wait(eng, s, per_channel, i, k, const=0):
            v = i * (per_channel * SLOTS) + (per_channel * k + const)
            if not isinstance(v, int) or v > 0:
                eng.wait_ge(s, v)

        def count(per_channel, i, k, const=0):
            return i * (per_channel * SLOTS) + (per_channel * k + const)

        XDMA = 16 * B
        TLDMA = 16 * RC * 2

        def first_of(i, k):
            return isinstance(i, int) and i == 0 and k == 0

        def past_end(i, k):
            return isinstance(i, int) and i * SLOTS + k >= C

        @block.sync
        def _(sp):
            def held(value):
                return value if isinstance(value, int) else sp.compute_val(value)

            def held_address(elements, size):
                at = held(elements)
                held(at * size)
                return at

            def wait_held(s, value):
                if not isinstance(value, int) or value > 0:
                    sp.wait_ge(s, value)

            def plane(t, b, at):
                return bass.AP(t.tensor, at + b * C * H * W, [[ROW, CR], [1, ROW]])

            def load_x(i, k):
                s = k % SLOTS
                at = held_address((i * SLOTS + k) * (H * W), 4)
                before = held(count(0, 0, 0, (i + k // SLOTS) * XDMA))
                wait_held(stored[s], before)
                if isinstance(i, int) and i == 0 and k < SLOTS:
                    sp.wait_ge(x_clear[k], 1)
                    if k == SLOTS - 1:
                        sp.wait_ge(zero_rest_in, 16 * ZPIECES)
                for b in range(B):
                    h, bb = b // IMG, b % IMG
                    sp.dma_start(X[PITCH * bb:PITCH * bb + CR, s, h, :], plane(x, b, at)).then_inc(x_in[s], 16)

            def store_x(i, k):
                s = k % SLOTS
                at = held_address((i * SLOTS + k) * (H * W), 4)
                full = held(count(1, i, k, 1))
                wait_held(xadd_done, full)
                for b in range(B):
                    h, bb = b // IMG, b % IMG
                    sp.dma_start(plane(out, b, at), X[PITCH * bb:PITCH * bb + CR, s, h, :]).then_inc(stored[s], 16)

            def load_matrices(i, t, rows=range(RC)):
                corner = PAD_R * TAB_C * CELL
                at = held_address((i + t) * (4 * TAB_R * TAB_C * CELL) + corner, 2)
                packed = held(count(1, i + t, 0))
                wait_held(tw_done, packed)
                for r in rows:
                    for pc in range(2):
                        fixed = ((2 * (r % 2) + pc) * TAB_R - 2 * (r // 2)) * TAB_C * CELL
                        src = bass.AP(table, at + fixed, [[2 * CELL, CC // 2], [TAB_C * CELL, WIN_R],
                                                          [1, WIN_C * CELL]])
                        dst = TL[CC * r + pc:CC * r + CC:2, :, :, :, :, :]
                        sp.dma_start(dst.rearrange("p r c l a s -> p r (c l a s)"), src).then_inc(tl_in, 16)

            def d1_move(i, k):
                v, w = held(count(1, i, k, 1)), held(count(1, i, k))
                wait_held(d1_done, v)
                wait_held(b1_done, w)
                wait_held(d2_done, w)
                for h in range(HALVES):
                    sp.dma_start(D1p[64 * h:64 * h + 64, :], D1[:, h, :]).then_inc(d1p_in, 16)

            def d2_move(i, k):
                v, w = held(count(1, i, k, 1)), held(count(1, i, k))
                wait_held(d2_done, v)
                wait_held(b2_done, w)
                sp.dma_start(D2p[:, :], D2[:, :]).then_inc(d2p_in, 16)

            def n2_move(i, k):
                v, w = held(count(1, i, k, 1)), held(count(1, i, k))
                wait_held(n2q_done, v)
                wait_held(n1r_done, w)
                sp.dma_start(N2m[:, :], N2q[:, :]).then_inc(n2m_in, 16)

            def n1_move(i, k):
                v, w = held(count(1, i, k, 1)), held(count(1, i, k))
                wait_held(n1r_done, v)
                wait_held(xadd_done, w)
                for h in range(HALVES):
                    sp.dma_start(N1m[:, h, :], N1r[64 * h:64 * h + 64, :]).then_inc(n1m_in, 16)

            sp.dma_start(WCf.rearrange("c (l n) -> c l n", l=LV),
                         wconv_w.rearrange("l (c s) a b -> c l (s a b)", s=4)).then_inc(weights_in, 16)
            sp.dma_start(BWf, base_w.rearrange("c a b -> c (a b)")).then_inc(weights_in, 16)
            sp.dma_start(WSf.rearrange("c (l n) -> c l n", l=LV),
                         wscale.rearrange("l (c s) -> c l s", s=4)).then_inc(weights_in, 16)
            sp.dma_start(BSf, base_scale.rearrange("(c o) -> c o", o=1)).then_inc(weights_in, 16)
            sp.dma_start(ident[:, :], ident_c).then_inc(consts_in, 16)
            sp.dma_start(avg[:, :], avg_c).then_inc(consts_in, 16)
            sp.dma_start(mask[:, :], mask_c).then_inc(consts_in, 16)
            sp.dma_start(bias[:, :], base_b.partition_broadcast(128)).then_inc(consts_in, 16)
            flat = table.ap().rearrange("g q r c n -> g (q r c n)")
            sp.wait_ge(x_clear[SLOTS - 1], 1)
            sp.dma_start(flat[0].rearrange("(p n) -> p n", p=ZP), zeros[:, 0:zero_first]).then_inc(zero_first_in, 16)
            for k in range(GC):
                load_x(0, k)

            def write_table(turns, s):
                for t in turns:
                    for q in range(4):
                        stored_q = 2 * (q // 2) + 1 - q % 2
                        dst = table.ap()[t, stored_q, PAD_R:PAD_R + PATCH, PAD_C:PAD_C + PATCH, :]
                        sp.dma_start(dst, ZT[:, q, t, :, :, :].rearrange("p l a s -> p (l a s)")).then_inc(s, 16)

            sp.wait_ge(zero_first_in, 16)
            sp.wait_ge(z_low, LV)
            write_table([0], table_first)
            sp.wait_ge(table_first, 16 * 4)
            load_matrices(0, 0)
            load_x(0, GC)
            d1_move(0, 0)
            d2_move(0, 0)
            rest = flat[1:TURNS].rearrange("g n -> (g n)").rearrange("(a p n) -> a p n", a=ZPIECES, p=ZP)
            for a in range(ZPIECES):
                sp.dma_start(rest[a], zeros[:, 0:zero_rest]).then_inc(zero_rest_in, 16)

            TABLE_AT = {0: (2, 5), 1: (5, 9), 2: (9, 13), 5: (13, TURNS)}

            def turn(i):
                for k in range(SLOTS):
                    if not first_of(i, k):
                        n1_move(i, k - 1)
                    if not past_end(i, k + 4):
                        load_x(i, k + 4)
                    if not past_end(i, k + 1):
                        d1_move(i, k + 1)
                    matrices = k == SLOTS - 2 and not past_end(i + 1, 0)
                    if matrices:
                        if isinstance(i, int):
                            sp.wait_ge(table_second, 16 * 4)
                        else:
                            sp.wait_ge(table_rest, 16 * 4 * (TURNS - 2))
                        load_matrices(i, 1, range(0, RC // 2))
                    n2_move(i, k)
                    if not past_end(i, k + 1):
                        d2_move(i, k + 1)
                    if matrices:
                        load_matrices(i, 1, range(RC // 2, RC))
                    if not first_of(i, k):
                        store_x(i, k - 1)
                    if isinstance(i, int) and i == 0 and k in TABLE_AT:
                        if k == 0:
                            write_table([1], table_second)
                        write_table(range(*TABLE_AT[k]), table_rest)

            turn(0)
            with sp.Fori(1, TURNS - 1) as i:
                turn(i)
            turn(TURNS - 1)
            n1_move(TURNS, -1)
            sp.wait_ge(last_half, 1)
            store_x(TURNS, -1)
            for s in range(SLOTS):
                sp.wait_ge(stored[s], TURNS * XDMA)

        @block.gpsimd
        def _(pool):
            for s in (5, 2):
                nc.gpsimd.memset(X[:, s, :, :], 0.0).then_inc(x_clear[s], 1)
            for t in (XH, XL):
                nc.gpsimd.memset(t[:, :, :, :], 0.0).then_inc(pads_clear, 1)
            nc.gpsimd.memset(X[:, 3, :, :], 0.0).then_inc(x_clear[3], 1)
            for t in (XH1, XL1, XH2, XL2):
                nc.gpsimd.memset(t[:, :, :], 0.0).then_inc(pads_clear, 1)
            nc.gpsimd.memset(B2[:, :, :, :], 0.0).then_inc(pads_clear, 1)

            def d1_sum(i, k):
                wait(pool, xn_done, 1, i, k, 1)
                wait(pool, d1p_in, 32, i, k)
                for h in range(HALVES):
                    if h == 0:
                        wait(pool, d1_done, 1, i, k)
                    else:
                        wait(pool, rs_done, 3, i, k, 2)
                    v = XN[:, k % 2, h, :].rearrange("p (jr two c) -> p jr two c", two=2, c=CC)
                    nc.gpsimd.tensor_tensor(RS[:, :].rearrange("p (jr c) -> p jr c", c=CC), v[:, :, 0, :],
                                            v[:, :, 1, :], ALU.add).then_inc(rs_done, 1)
                    wait(pool, rs_done, 3, i, k, 2 * h + 1)
                    t = RS[:, :].rearrange("p (j r q two) -> p r j q two", j=NB, r=4, two=2)
                    o = D1[:, h, :].rearrange("p (r j q) -> p r j q", r=4, q=CC // 2)[:, :, :, ::-1]
                    nc.gpsimd.tensor_tensor(o, t[:, :, :, :, 0], t[:, :, :, :, 1],
                                            ALU.add).then_inc(d1_done if h else rs_done, 1)

            def d2_sum(i, k):
                wait(pool, d1p_in, 32, i, k, 32)
                wait(pool, d2p_in, 16, i, k)
                v = D1p[:, :].rearrange("p (r two c) -> p r two c", two=2, c=HC)
                nc.gpsimd.tensor_tensor(RS2[:, :].rearrange("p (r c) -> p r c", r=4), v[:, :, 0, :], v[:, :, 1, :],
                                        ALU.add).then_inc(rs2_done, 1)
                wait(pool, rs2_done, 1, i, k, 1)
                t = RS2[:, :].rearrange("p (n two) -> p n two", two=2)
                nc.gpsimd.tensor_tensor(D2[:, :], t[:, :, 0], t[:, :, 1], ALU.add).then_inc(d2_done, 1)

            def up(v, cols):
                return v.rearrange("p (r c o) -> p r c o", r=4, o=1).to_broadcast([128, 4, cols, 2])

            def n1_add(i, k):
                wait(pool, n2m_in, 16, i, k, 16)
                wait(pool, n1r_evac, 1, i, k, 1)
                v = N1r[:, :].rearrange("p (r two c d) -> p r two c d", two=2, c=HC // 2, d=2)
                for a in range(2):
                    op = nc.gpsimd.tensor_tensor(v[:, :, a, :, :], v[:, :, a, :, :], up(N2m[:, :], HC // 2), ALU.add)
                op.then_inc(n1r_done, 1)

            def x_add(i, k):
                wait(pool, n1m_in, 32, i, k, 32)
                wait(pool, fin, 4, i, k, 4)
                for h in range(1 if isinstance(i, int) and i == TURNS else HALVES):
                    v = X[:, k % SLOTS, h, :].rearrange("p (r two c d) -> p r two c d", two=2, c=HC, d=2)
                    for a in range(2):
                        op = nc.gpsimd.tensor_tensor(v[:, :, a, :, :], v[:, :, a, :, :], up(N1m[:, h, :], HC), ALU.add)
                op.then_inc(xadd_done, 1)

            d1_sum(0, 0)
            d2_sum(0, 0)

            def turn(i):
                for k in range(SLOTS):
                    if not first_of(i, k):
                        n1_add(i, k - 1)
                    if not past_end(i, k + 1):
                        d1_sum(i, k + 1)
                    if not first_of(i, k):
                        x_add(i, k - 1)
                    if not past_end(i, k + 1):
                        d2_sum(i, k + 1)

            turn(0)
            with pool.Fori(1, TURNS - 1) as i:
                turn(i)
            turn(TURNS - 1)
            n1_add(TURNS, -1)
            x_add(TURNS, -1)

        EDGES = [0, 56, 120, 168, W]

        def bank_columns(u):
            if u < 4:
                e = EDGES[2 * (u % 2):2 * (u % 2) + 3]
                return [(e[0], e[1]), (e[1], e[2])]
            return [(0, 56)] if u == 4 else [(0, 56), (56, HC)]

        def bank_view(bank, c0, c1):
            return bank[:, 0:RC * (c1 - c0)].rearrange("p (r w) -> p r w", r=RC)

        def split_dst(u, hi):
            if u < 4:
                h, c = u // 2, u % 2
                return (XH if hi else XL)[:, h, HB * c:HB * c + HB, 1:129]
            if u == 4:
                return (XH2 if hi else XL2)[:, :, 1:65]
            return (XH1 if hi else XL1)[:, :, 1:129]

        def banks(u):
            return [(0, 2), (2, 4)] if u == 4 else [(0, 4), (4, 7)]

        def rows_of(u):
            return 64 if u == 4 else 128

        def split_wait(eng, u, i, k):
            last = (2, 2, 4, 4, 5, 6)[u] - UNITS
            wait(eng, mm_done, UNITS, i, k, last)

        @block.scalar
        def _(act):
            for s in (1, 4):
                nc.scalar.memzero(X[:, s, :, :]).then_inc(x_clear[s], 1)
            for lv in range(LV):
                act.wait_ge(z_turned, lv + 1)
                src = S[lv // 2][lv % 2][0:PATCH * PATCH, 0:4 * C].rearrange("p (t s) -> p t s", s=SLOTS)
                dst = ZT[:, :, :, lv, 0, :].rearrange("p q t s -> p (q t) s")
                nc.scalar.activation(dst, src, ACT.Copy).then_inc(z_high, 1)

            def high_part(i, k, u):
                split_wait(act, u, i, k)
                for b, (j0, j1) in enumerate(banks(u)):
                    wait(act, turned, 2 * UNITS, i, k, 2 * u + b + 1)
                    src = S[u % 2][b][:, 0:(j1 - j0) * 128].rearrange("p (j m) -> p j m", m=128)[:, :, 0:rows_of(u)]
                    nc.scalar.activation(split_dst(u, True)[:, j0:j1, :], src, ACT.Copy).then_inc(high, 1)

            def pack(i, k, lv):
                if lv == 0:
                    act.wait_ge(tl_in, (i + k // SLOTS + 1) * TLDMA)
                    wait(act, mm_done, UNITS, i, k - 1)
                src = TL[:, :, :, lv, :, k % SLOTS].rearrange("p r c a -> p a (r c)")
                dst = TW[:, k % 2, lv, :, :, :].rearrange("p a r c -> p a (r c)")
                op = nc.scalar.activation(dst, src, ACT.Copy)
                if lv == LV - 1:
                    op.then_inc(tw_done, 1)

            def b1_copy(i, k):
                wait(act, d1p_in, 32, i, k, 32)
                wait(act, turned, 2 * UNITS, i, k - 1, 2 * UNITS)
                src = D1p[:, :].rearrange("p (r j c) -> p r j c", r=RC, c=CC)
                dst = B1[:, :].rearrange("p (j r c) -> p r j c", r=RC, c=CC)[:, :, :, ::-1]
                nc.scalar.activation(dst, src, ACT.Copy).then_inc(b1_done, 1)

            def b2_copy(i, k):
                wait(act, d2p_in, 16, i, k, 16)
                wait(act, turned, 2 * UNITS, i, k - 1, 2 * UNITS - 2)
                v = D2p[:, :].rearrange("p (r c) -> p r c", r=RC)
                src = v[:, :, 0:48].rearrange("p r (j c) -> p r j c", c=CC)
                dst = B2[0:64, 0:3, :, :].rearrange("p j r c -> p r j c")[:, :, :, ::-1]
                nc.scalar.activation(dst, src, ACT.Copy)
                nc.scalar.activation(B2[0:64, 3, :, 8:16][:, :, ::-1], v[:, :, 48:56], ACT.Copy).then_inc(b2_done, 1)

            def n2_evac(i, k):
                wait(act, mm_done, UNITS, i, k, 5)
                wait(act, n2m_in, 16, i, k)
                nc.scalar.activation(N2q[:, :], O[0][0][0:64, 0:Q4], ACT.Copy,
                                     scale=0.25 / (4 * S_X * S_W)).then_inc(n2q_done, 1)

            def n1_evac(i, k):
                wait(act, mm_done, UNITS, i, k, 6)
                wait(act, n1m_in, 32, i, k)
                for b, (b0, b1) in enumerate(bank_columns(5)):
                    dst = N1r[:, :].rearrange("p (r w) -> p r w", r=RC)[:, :, b0:b1]
                    op = nc.scalar.activation(dst, bank_view(O[1][b], b0, b1), ACT.Identity,
                                              scale=0.5 / (2 * S_X * S_W), bias=bias[:, bass.ds(i * SLOTS + k, 1)])
                op.then_inc(n1r_evac, 1)

            def root():
                nc.scalar.activation(SQ[:, 1, :], SQ[:, 0, :], ACT.Sqrt).then_inc(root_done, 1)

            act.wait_ge(var_first, 1)
            root()
            act.wait_ge(pads_clear, 7)
            act.wait_ge(consts_in, 64)
            for u in range(AHEAD):
                high_part(0, 0, u)
            for lv in range(LV):
                pack(0, 0, lv)

            def turn(i):
                for k in range(SLOTS):
                    for u in range(UNITS):
                        v = u + AHEAD
                        if not past_end(i, k + v // UNITS):
                            high_part(i, k + v // UNITS, v % UNITS)
                        if v == VAR_UNIT and k % GC == GC - 1 and not past_end(i, k + 1):
                            wait(act, low, 2 * UNITS, i, k, 2 * v + 2)
                            root()
                        if k < SLOTS - 1 and u < LV:
                            pack(i, k + 1, u)
                        if k == SLOTS - 1 and u >= UNITS - LV and not past_end(i, k + 1):
                            pack(i, k + 1, u - (UNITS - LV))
                        if u == 0:
                            b2_copy(i, k)
                        if u == 1:
                            b1_copy(i, k)
                        if u == 4:
                            n2_evac(i, k)
                    n1_evac(i, k)

            turn(0)
            with act.Fori(1, TURNS - 1) as i:
                turn(i)
            turn(TURNS - 1)

        @block.vector
        def _(dve):
            links = [0]

            def link(op):
                links[0] += 1
                op.then_inc(chain, 1)
                dve.wait_ge(chain, links[0])

            nc.vector.memset(X[:, 0, :, :], 0.0).then_inc(x_clear[0], 1)

            dve.wait_ge(weights_in, 64)
            WC = WCf.rearrange("c (ls n) -> c ls n", n=25)
            link(nc.vector.tensor_tensor(WC, WC, WSf.rearrange("c (ls o) -> c ls o", o=1)
                                         .to_broadcast([C, LV * 4, 25]), ALU.mult))
            W4 = WCf.rearrange("c (lp two n) -> c lp two n", two=2, n=25)
            A4 = AAf.rearrange("c (lp two n) -> c lp two n", two=2, n=25)
            link(nc.vector.tensor_tensor(A4[:, :, 0, :], W4[:, :, 0, :], W4[:, :, 1, :], ALU.add))
            link(nc.vector.tensor_tensor(A4[:, :, 1, :], W4[:, :, 0, :], W4[:, :, 1, :], ALU.subtract))
            A2 = AAf.rearrange("c (l two n) -> c l two n", l=LV, two=2)
            H2 = HHf.rearrange("c (l two n) -> c l two n", l=LV, two=2)
            link(nc.vector.tensor_tensor(H2[:, :, 0, :], A2[:, :, 0, :], A2[:, :, 1, :], ALU.add))
            link(nc.vector.tensor_tensor(H2[:, :, 1, :], A2[:, :, 0, :], A2[:, :, 1, :], ALU.subtract))
            HV = HHf.rearrange("c (l x a b) -> c l x a b", l=LV, x=4, a=KS)
            Z = ZZf.rearrange("c (l q a b) -> c l q a b", l=LV, q=4, a=PATCH)
            for q in range(4):
                for o in range(4):
                    link(nc.vector.tensor_scalar(Z[:, :, q, o // 2::2, o % 2::2], HV[:, :, q ^ o, :, :],
                                                 0.25 * S_W, None, ALU.mult))
            BW = BWf.rearrange("c (a b) -> c a b", a=KS)
            link(nc.vector.tensor_scalar(BWf, BWf, BSf, S_W, ALU.mult, ALU.mult))
            for q in range(4):
                t = Z[:, 0, q, q // 2 + 2:q // 2 + 2 + KS, q % 2 + 2:q % 2 + 2 + KS]
                op = nc.vector.tensor_tensor(t, t, BW, ALU.add)
                if q == 3:
                    op.then_inc(z_ready, 1)
                else:
                    link(op)
            for lv in range(LV):
                dve.wait_ge(z_high, lv + 1)
                src = S[lv // 2][lv % 2][0:PATCH * PATCH, 0:4 * C].rearrange("p (t s) -> p t s", s=SLOTS)
                z = ZT[:, :, :, lv, :, :].rearrange("p q t a s -> p (q t) a s")
                nc.vector.tensor_tensor(z[:, :, 1, :], src, z[:, :, 0, :], ALU.subtract).then_inc(z_low, 1)

            def chan_stats(i, k, h):
                dve.wait_ge(x_in[k % SLOTS], (i + k // SLOTS + 1) * XDMA)
                for c in range(4):
                    op = nc.vector.bn_stats(ST[:, h, 4 * (k % GC) + c, :], X[:, k % SLOTS, h, c * Q4:(c + 1) * Q4])
                return op

            STEPS = 8

            def step(op, i, gk, n):
                op.then_inc(stat_step, 1)
                dve.wait_ge(stat_step, i * (2 * STEPS) + (gk * STEPS + n))

            def stats_mean(last, i, gk):
                step(last, i, gk, 1)
                nc.vector.memset(spare[:, :], 0.0)
                for h in range(HALVES):
                    op = nc.vector.bn_aggr(MV[:, h, :], ST[:, h, :, :].rearrange("p a b -> p (a b)"))
                op.then_inc(mv_ready, 1)

            def take_mean(bank):
                return nc.vector.tensor_copy(GM[:, :], bank[:, MEAN_AT:MEAN_AT + HALVES])

            def stats_var(i, gk):
                step(nc.vector.tensor_tensor(SQ[:, 0, :], MV[:, :, 0], GM[:, :], ALU.subtract), i, gk, 2)
                step(nc.vector.tensor_tensor(SQ[:, 1, :], SQ[:, 0, :], SQ[:, 0, :], ALU.mult), i, gk, 3)
                nc.vector.tensor_tensor(SQ[:, 2, :], SQ[:, 1, :], MV[:, :, 1], ALU.add).then_inc(vq_ready, 1)

            def take_var(bank):
                return nc.vector.tensor_scalar(SQ[:, 0, :], bank[:, VAR_AT:VAR_AT + HALVES], EPS, None, ALU.add)

            def stats_scale(i, gk):
                dve.wait_ge(root_done, i * 2 + (gk + 1))
                step(nc.vector.reciprocal(SQ[:, 1, :], SQ[:, 1, :]), i, gk, 4)
                step(nc.vector.tensor_tensor(SQ[:, 3, :], SQ[:, 1, :], SQ[:, 1, :], ALU.mult), i, gk, 5)
                step(nc.vector.tensor_tensor(SQ[:, 3, :], SQ[:, 3, :], SQ[:, 0, :], ALU.mult), i, gk, 6)
                step(nc.vector.tensor_scalar(SQ[:, 3, :], SQ[:, 3, :], -0.5, 1.5, ALU.mult, ALU.add), i, gk, 7)
                step(nc.vector.scalar_tensor_tensor(RG[:, :], SQ[:, 1, :], mask[:, 0:1], SQ[:, 3, :], ALU.mult,
                                                    ALU.mult), i, gk, 8)

            def normalise(i, k):
                wait(dve, turned, 2 * UNITS, i, k - 2, 8)
                wait(dve, d1_done, 1, i, k - 1)
                for h in range(HALVES):
                    src = X[:, k % SLOTS, h, :].rearrange("p (r j c) -> p r j c", r=RC, c=CC)
                    dst = XN[:, k % 2, h, :].rearrange("p (j r c) -> p r j c", r=RC, c=CC)[:, :, :, ::-1]
                    op = nc.vector.tensor_scalar(dst, src, GM[:, h:h + 1], RG[:, h:h + 1], ALU.subtract, ALU.mult)
                op.then_inc(xn_done, 1)

            def low_part(i, k, u):
                for b, (j0, j1) in enumerate(banks(u)):
                    wait(dve, high, 2 * UNITS, i, k, 2 * u + b + 1)
                    src = S[u % 2][b][:, 0:(j1 - j0) * 128].rearrange("p (j m) -> p j m", m=128)[:, :, 0:rows_of(u)]
                    op = nc.vector.tensor_tensor(split_dst(u, False)[:, j0:j1, :], src,
                                                 split_dst(u, True)[:, j0:j1, :], ALU.subtract)
                    if b == 0:
                        op.then_inc(low, 1)
                return op

            def final(i, k, u):
                wait(dve, mm_done, UNITS, i, k, u + 1)
                for b, (b0, b1) in enumerate(bank_columns(u)):
                    t = X[:, k % SLOTS, u // 2, :].rearrange("p (r w) -> p r w", r=RC)[:, :, b0:b1]
                    op = nc.vector.scalar_tensor_tensor(t, bank_view(O[u % 2][b], b0, b1),
                                                        1.0 / (S_X * S_W), t, ALU.mult, ALU.add)
                op.then_inc(fin, 1)

            dve.wait_ge(consts_in, 64)
            for k in range(GC):
                for h in range(HALVES):
                    last = chan_stats(0, k, h)
            stats_mean(last, 0, 0)
            dve.wait_ge(stat_mm, 1)
            link(take_mean(S[1][1]))
            stats_var(0, 0)
            dve.wait_ge(stat_mm, 2)
            take_var(S[1][1]).then_inc(var_first, 1)
            stats_scale(0, 0)
            normalise(0, 0)
            dve.wait_ge(pads_clear, 7)
            for u in range(AHEAD):
                low_part(0, 0, u).then_inc(low, 1)

            def turn(i):
                for k in range(SLOTS):
                    kk, gk = k % GC, k // GC + 1
                    more = not past_end(i, k - kk + GC)
                    if kk == GC - 1 and more:
                        stats_mean(last_stats, i, gk)
                    if kk < GC - 1:
                        normalise(i, k + 1)
                    for u in range(UNITS):
                        v = u + AHEAD
                        if not past_end(i, k + v // UNITS):
                            last = low_part(i, k + v // UNITS, v % UNITS)
                            if more and kk == GC - 1 and v in (MEAN_UNIT, VAR_UNIT):
                                take = take_mean if v == MEAN_UNIT else take_var
                                take(S[v % 2][1]).then_inc(low, 1)
                                wait(dve, low, 2 * UNITS, i, k, 2 * v + 2)
                                if v == MEAN_UNIT:
                                    stats_var(i, gk)
                                else:
                                    stats_scale(i, gk)
                                    normalise(i, k + 1)
                            else:
                                last.then_inc(low, 1)
                        if more and kk < GC - 1 and u in (1, 2):
                            chan_stats(i, k + GC, u - 1)
                        if more and kk == GC - 2 and u in (3, 4):
                            last_stats = chan_stats(i, k + GC + 1, u - 3)
                        if u < 4:
                            final(i, k, u)

            turn(0)
            with dve.Fori(1, TURNS - 1) as i:
                turn(i)
            turn(TURNS - 1)
            wait(dve, n1m_in, 32, TURNS, -1, 32)
            wait(dve, fin, 4, TURNS, -1, 4)
            v = X[:, SLOTS - 1, 1, :].rearrange("p (r two c d) -> p r two c d", two=2, c=HC, d=2)
            n1 = N1m[:, 1, :].rearrange("p (r c o) -> p r c o", r=4, o=1).to_broadcast([128, 4, HC, 2])
            for a in range(2):
                op = nc.vector.tensor_tensor(v[:, :, a, :, :], v[:, :, a, :, :], n1, ALU.add)
            op.then_inc(last_half, 1)

        @block.tensor
        def _(pe):
            def average(i, gk, var, bank):
                pe.wait_ge(vq_ready if var else mv_ready, i * 2 + (gk + 1))
                rhs, at = (SQ[:, 2, :], VAR_AT) if var else (MV[:, :, 0], MEAN_AT)
                return nc.tensor.matmul(bank[:, at:at + HALVES], avg[:, :], rhs, start=True, stop=True)

            def transposes(i, k, u, stat=None):
                if u < 4:
                    wait(pe, xn_done, 1, i, k, 1)
                elif u == 4:
                    wait(pe, b2_done, 1, i, k, 1)
                else:
                    wait(pe, b1_done, 1, i, k, 1)
                for b, (j0, j1) in enumerate(banks(u)):
                    wait(pe, low, 2 * UNITS, i, k, 2 * (u - 2) + b + 1)
                    bank = S[u % 2][b]
                    for j in range(j0, j1):
                        if u < 4:
                            src = XN[:, k % 2, u // 2, 128 * (HB * (u % 2) + j):128 * (HB * (u % 2) + j) + 128]
                        elif u == 4:
                            src = B2[:, j, :, :].rearrange("p r c -> p (r c)")
                        else:
                            src = B1[:, 128 * j:128 * j + 128]
                        op = nc.tensor.transpose(bank[:, (j - j0) * 128:(j - j0) * 128 + 128], src, ident[:, :])
                    if b == 1 and stat is not None:
                        op = average(i, stat[0], stat[1], bank)
                    op.then_inc(turned, 1)

            def products(i, k, u):
                if u < 4:
                    lv = 0
                    hi, lo = XH[:, u // 2, :, :], XL[:, u // 2, :, :]
                    nblk = NB
                    wait(pe, low, 2 * UNITS, i, k, 2 * (u // 2 * 2 + 2))
                elif u == 4:
                    lv, nblk, hi, lo = 2, 4, XH2, XL2
                    wait(pe, low, 2 * UNITS, i, k, 2 * u + 2)
                else:
                    lv, nblk, hi, lo = 1, HB, XH1, XL1
                    wait(pe, low, 2 * UNITS, i, k, 2 * u + 2)
                m = rows_of(u)
                if u == 0:
                    wait(pe, n2q_done, 1, i, k)
                elif u == 1:
                    wait(pe, n1r_evac, 1, i, k)
                else:
                    wait(pe, fin, 4, i, k, u - 1)
                if u == 0:
                    wait(pe, tw_done, 1, i, k, 1)
                columns = bank_columns(u)
                nbank = len(columns)
                begun = [False, False]

                def product(b, j, part, wp, dy, rows):
                    b0, b1 = columns[b]
                    a0, a1 = max(CC * j - REACH, b0), min(CC * j - REACH + WIN_C, b1)
                    w0 = a0 - (CC * j - REACH)
                    o0, o1 = {0: (0, RC), -1: (0, REACH), 1: (RC - REACH, RC)}[dy]
                    r0 = o0 + REACH - RC * dy
                    lhs = (lo if part else hi)[rows, j, 1 + dy:1 + dy + m]
                    rhs = TW[rows, k % 2, lv, wp, r0:r0 + o1 - o0, w0:w0 + a1 - a0]
                    dst = bank_view(O[u % 2][b], b0, b1)[0:m]
                    op = nc.tensor.matmul(dst[:, o0:o1, a0 - b0:a1 - b0], lhs, rhs, start=not begun[b], stop=True,
                                          skip_group_check=True)
                    begun[b] = True
                    return op

                def blocks(b):
                    b0, b1 = columns[b]
                    return [j for j in range(nblk) if CC * j - REACH < b1 and CC * j - REACH + WIN_C > b0]

                every = slice(0, 128)
                top, bottom = (slice(0, 64), slice(64, 128)) if m == 128 else (every, every)

                def own_cells(js):
                    for j in js:
                        for part in range(2):
                            for b in range(nbank):
                                if j in blocks(b):
                                    for wp in range(2 - part):
                                        product(b, j, part, wp, 0, every)

                def other_cells(b):
                    above, below = blocks(b), blocks(nbank - 1 - b)
                    for n in range(max(len(above), len(below))):
                        for part in range(2):
                            for wp in range(2 - part):
                                if n < len(above):
                                    op = product(b, above[n], part, wp, -1, bottom)
                                if n < len(below):
                                    op = product(nbank - 1 - b, below[n], part, wp, 1, top)
                    return op

                own = sorted({j for b in range(nbank) for j in blocks(b)})
                for b in range(nbank):
                    own_cells(own[len(own) * b // nbank:len(own) * (b + 1) // nbank])
                    if b == 1:
                        wait(pe, round_done, UNITS - 1, i, k, min(u, 4) + 1)
                    op = other_cells(b)
                    if b < nbank - 1:
                        op.then_inc(round_done, 1)
                op.then_inc(mm_done, 1)

            pe.wait_ge(consts_in, 64)
            pe.wait_ge(z_ready, 1)
            for lv in range(LV):
                for q in range(4):
                    n = PATCH * PATCH
                    op = nc.tensor.transpose(S[lv // 2][lv % 2][0:n, C * q:C * q + C],
                                             ZZf[:, (4 * lv + q) * n:(4 * lv + q + 1) * n], ident[0:C, 0:C])
                op.then_inc(z_turned, 1)
            average(0, 0, False, S[1][1]).then_inc(stat_mm, 1)
            average(0, 0, True, S[1][1]).then_inc(stat_mm, 1)
            pe.wait_ge(pads_clear, 7)
            pe.wait_ge(z_low, LV)
            for u in range(AHEAD):
                transposes(0, 0, u)

            def turn(i):
                for k in range(SLOTS):
                    kk, gk = k % GC, k // GC + 1
                    more = not past_end(i, k - kk + GC)
                    for u in range(UNITS):
                        v = u + AHEAD
                        if not past_end(i, k + v // UNITS):
                            stat = (gk, v == VAR_UNIT) if more and kk == GC - 1 and v in (MEAN_UNIT, VAR_UNIT) else None
                            transposes(i, k + v // UNITS, v % UNITS, stat)
                        products(i, k, u)

            turn(0)
            with pe.Fori(1, TURNS - 1) as i:
                turn(i)
            turn(TURNS - 1)


def kernel(x, L0_conv_base_w, L0_conv_base_b, L0_conv_base_scale, L0_conv_wconv_w, L0_conv_wscale):
    import numpy as np
    import concourse.bacc as bacc
    from concourse.bass_utils import run_bass_kernel_spmd

    f32 = np.float32
    B, C, H, W = x.shape
    L = L0_conv_wconv_w.shape[0]
    PITCH, CR = 32, H // 8
    row = np.arange(128)
    pixel = row % PITCH < CR
    avg = ((row[:, None] // PITCH == row[None, :] // PITCH) & pixel[:, None] & pixel[None, :]).astype(f32) / f32(CR)
    arrays = {
        "x": np.ascontiguousarray(x),
        "base_w": np.ascontiguousarray(L0_conv_base_w[:, 0, ::-1, ::-1]),
        "base_b": np.ascontiguousarray(L0_conv_base_b),
        "base_scale": np.ascontiguousarray(L0_conv_base_scale).reshape(C),
        "wconv_w": np.ascontiguousarray(L0_conv_wconv_w[:, :, 0, ::-1, ::-1]),
        "wscale": np.ascontiguousarray(L0_conv_wscale).reshape(L, 4 * C),
        "ident": np.eye(128, dtype=f32),
        "avg": avg,
        "mask": (pixel.astype(f32) * f32(4.0)).reshape(128, 1),
    }
    nc = bacc.Bacc("TRN2", target_bir_lowering=False, num_devices=1)
    f = mybir.dt.float32
    args = [nc.dram_tensor(f"in_{n}", a.shape, f, kind="ExternalInput").ap() for n, a in arrays.items()]
    out = nc.dram_tensor("out", (B, C, H, W), f, kind="ExternalOutput").ap()
    build(nc, *args, out)
    return run_bass_kernel_spmd(nc, [{f"in_{n}": a for n, a in arrays.items()}], core_ids=[0]).results[0]["out"]
```
